# Optimizing a Trainium2 kernel written in Bass

```python
import numpy as np
import jax
import jax.numpy as jnp

def _softmax(x, axis=-1):
    return jax.nn.softmax(x, axis=axis)

def _gelu(x):
    return jax.nn.gelu(x, approximate=True)

def _silu(x):
    return jax.nn.silu(x)

def _sigmoid(x):
    return jax.nn.sigmoid(x)

def _layernorm(x, axis=-1, eps=1e-05):
    m = jnp.mean(x, axis=axis, keepdims=True)
    v = jnp.var(x, axis=axis, keepdims=True)
    return (x - m) / jnp.sqrt(v + eps)

def _scatter_add(tgt, idx, src, axis=0):
    return tgt.at[idx].add(src)

def _segment_sum(src, seg, n):
    return jax.ops.segment_sum(src, seg, n)
kernel_name = 'mk_adj_ffn_d1_adj_r2_753cfb'

def setup_inputs(seed: int=0):
    np.random.seed(seed)
    _w = jnp.asarray

    def _rec_inputs():
        import jax
        import jax.numpy as jnp
        _gk = jax.random.key(seed)
        x = -0.0002928 + 1 * jax.random.normal(jax.random.fold_in(_gk, 1), (1354, 512), jnp.float32)
        _w = (1.0 + jnp.arange(1354, dtype=jnp.float32)) ** (-0.5)
        _w = _w / _w.mean()
        _pij = jnp.clip(0.00590842 * _w[:, None] * _w[None, :], 0.0, 1.0)
        _a = jax.random.uniform(jax.random.fold_in(_gk, 2), (1354, 1354)) < _pij
        _af = _a.astype(jnp.float32)
        adj = _af
        return (x, adj)
    x, adj = _rec_inputs()

    def _L0_gnn_setup():
        import jax, jax.numpy as jnp
        import numpy as np
        import math
        SENT_DIM = 512
        N_SENT = 2048
        key = jax.random.key(seed)
        ks = jax.random.split(key, 8)
        D = SENT_DIM
        s = 1.0 / math.sqrt(D)
        return {'sent_embed': jax.random.normal(ks[0], (N_SENT, D), dtype=jnp.float32), 'adj_tensor': jax.random.randint(ks[1], (N_SENT, N_SENT), 0, 2).astype(jnp.float32), 'W_q': jax.random.uniform(ks[2], (D, D), jnp.float32, -s, s), 'b_q': jax.random.uniform(ks[3], (D,), jnp.float32, -s, s), 'W_k': jax.random.uniform(ks[4], (D, D), jnp.float32, -s, s), 'b_k': jax.random.uniform(ks[5], (D,), jnp.float32, -s, s), 'W_v': jax.random.uniform(ks[6], (D, D), jnp.float32, -s, s), 'b_v': jax.random.uniform(ks[7], (D,), jnp.float32, -s, s)}
    _L0_gnn_all = _L0_gnn_setup()
    _L0_gnn_in = {k: v for k, v in _L0_gnn_all.items() if k in ('W_q', 'b_q', 'W_k', 'b_k', 'W_v', 'b_v')}
    del _L0_gnn_all

    def _L0_ffn_setup():
        import jax, jax.numpy as jnp
        import numpy as np
        EPS = 1e-05

        def _layernorm(x, w, b):
            mu = jnp.mean(x, axis=-1, keepdims=True)
            var = jnp.mean((x - mu) ** 2, axis=-1, keepdims=True)
            return (x - mu) * jax.lax.rsqrt(var + EPS) * w + b

        def _rope_tables(T, D, base=10000.0):
            inv_freq = 1.0 / base ** (jnp.arange(0, D, 2, dtype=jnp.float32) / D)
            t = jnp.arange(T, dtype=jnp.float32)
            freqs = jnp.einsum('i,j->ij', t, inv_freq)
            emb = jnp.concatenate([freqs, freqs], axis=-1)
            return (jnp.cos(emb), jnp.sin(emb))

        def _rotate_half(x):
            x1, x2 = (x[..., :x.shape[-1] // 2], x[..., x.shape[-1] // 2:])
            return jnp.concatenate([-x2, x1], axis=-1)

        def _attn(x, ln_w, ln_b, conv_w, attn_w, proj_w, n_head):
            B, T, C = x.shape
            D = C // n_head
            h = _layernorm(x, ln_w, ln_b)
            hc = jnp.transpose(h, (0, 2, 1))
            hc = jnp.pad(hc, ((0, 0), (0, 0), (2, 0)))
            hc = jax.lax.conv_general_dilated(hc, conv_w, window_strides=(1,), padding='VALID', dimension_numbers=('NCH', 'OIH', 'NCH'), feature_group_count=C)
            h = jnp.transpose(hc, (0, 2, 1))
            qkv = h @ attn_w
            q, k, v = jnp.split(qkv, 3, axis=-1)
            q = q.reshape(B, T, n_head, D)
            k = k.reshape(B, T, n_head, D)
            v = v.reshape(B, T, n_head, D)
            cos, sin = _rope_tables(T, D)
            cos = cos[None, :, None, :]
            sin = sin[None, :, None, :]
            q = q * cos + _rotate_half(q) * sin
            k = k * cos + _rotate_half(k) * sin
            scores = jnp.einsum('bqhd,bkhd->bhqk', q, k) / jnp.sqrt(jnp.float32(D))
            causal = jnp.tril(jnp.ones((T, T), dtype=bool))
            scores = jnp.where(causal, scores, jnp.float32(-1e+30))
            p = jax.nn.softmax(scores, axis=-1)
            y = jnp.einsum('bhqk,bkhd->bqhd', p, v).reshape(B, T, C)
            return y @ proj_w

        def _moe(x, ln_w, ln_b, router_w, expert_wv, expert_proj):
            h = _layernorm(x, ln_w, ln_b)
            logits = h @ router_w
            expert_idx = jnp.argmax(logits, axis=-1)
            E = router_w.shape[-1]
            out = jnp.zeros_like(x)
            for e in range(E):
                gv = h @ expert_wv[e]
                gate_raw, value = jnp.split(gv, 2, axis=-1)
                y = gate_raw * jax.nn.sigmoid(gate_raw) * value @ expert_proj[e]
                out = out + jnp.where((expert_idx == e)[..., None], y, 0.0)
            return out
        C, H, E, B, T = (512, 16, 4, 4, 512)
        Dff = 4 * C
        key = jax.random.key(seed)
        ks = jax.random.split(key, 8)
        s = 0.02
        return {'x': jax.random.normal(ks[0], (B, T, C), dtype=jnp.float32), 'ln1_w': jnp.ones((C,), jnp.float32), 'ln1_b': jnp.zeros((C,), jnp.float32), 'ln2_w': jnp.ones((C,), jnp.float32), 'ln2_b': jnp.zeros((C,), jnp.float32), 'conv_w': jax.random.normal(ks[1], (C, 1, 3), dtype=jnp.float32) * 0.1, 'attn_w': jax.random.normal(ks[2], (C, 3 * C), dtype=jnp.float32) * s, 'proj_w': jax.random.normal(ks[3], (C, C), dtype=jnp.float32) * s, 'router_w': jax.random.normal(ks[4], (C, E), dtype=jnp.float32) * s, 'expert_wv': jax.random.normal(ks[5], (E, C, 2 * Dff), dtype=jnp.float32) * s, 'expert_proj': jax.random.normal(ks[6], (E, Dff, C), dtype=jnp.float32) * s}
    _L0_ffn_all = _L0_ffn_setup()
    _L0_ffn_in = {k: v for k, v in _L0_ffn_all.items() if k in ('ln1_w', 'ln1_b', 'ln2_w', 'ln2_b', 'conv_w', 'attn_w', 'proj_w', 'router_w', 'expert_wv', 'expert_proj')}
    del _L0_ffn_all
    return {'x': x, 'adj': adj, 'L0_gnn_W_q': _L0_gnn_in['W_q'], 'L0_gnn_b_q': _L0_gnn_in['b_q'], 'L0_gnn_W_k': _L0_gnn_in['W_k'], 'L0_gnn_b_k': _L0_gnn_in['b_k'], 'L0_gnn_W_v': _L0_gnn_in['W_v'], 'L0_gnn_b_v': _L0_gnn_in['b_v'], 'L0_ffn_ln1_w': _L0_ffn_in['ln1_w'], 'L0_ffn_ln1_b': _L0_ffn_in['ln1_b'], 'L0_ffn_ln2_w': _L0_ffn_in['ln2_w'], 'L0_ffn_ln2_b': _L0_ffn_in['ln2_b'], 'L0_ffn_conv_w': _L0_ffn_in['conv_w'], 'L0_ffn_attn_w': _L0_ffn_in['attn_w'], 'L0_ffn_proj_w': _L0_ffn_in['proj_w'], 'L0_ffn_router_w': _L0_ffn_in['router_w'], 'L0_ffn_expert_wv': _L0_ffn_in['expert_wv'], 'L0_ffn_expert_proj': _L0_ffn_in['expert_proj']}

def reference(x, adj, L0_gnn_W_q, L0_gnn_b_q, L0_gnn_W_k, L0_gnn_b_k, L0_gnn_W_v, L0_gnn_b_v, L0_ffn_ln1_w, L0_ffn_ln1_b, L0_ffn_ln2_w, L0_ffn_ln2_b, L0_ffn_conv_w, L0_ffn_attn_w, L0_ffn_proj_w, L0_ffn_router_w, L0_ffn_expert_wv, L0_ffn_expert_proj):
    import jax
    import jax.numpy as jnp

    def _L0_gnn_ref(sent_embed, adj_tensor, W_q, b_q, W_k, b_k, W_v, b_v):
        import jax, jax.numpy as jnp
        import numpy as np
        import math
        SENT_DIM = 512
        N_SENT = 2048
        q = sent_embed @ W_q.T + b_q
        k = sent_embed @ W_k.T + b_k
        v = sent_embed @ W_v.T + b_v
        scale = 1.0 / math.sqrt(sent_embed.shape[-1])
        z = scale * (q @ k.T)
        spare_z = z * adj_tensor
        spare_z = jnp.where(spare_z == 0.0, jnp.asarray(-10000.0, spare_z.dtype), spare_z)
        attn = jax.nn.softmax(spare_z, axis=1)
        out = attn @ v
        return jax.nn.relu(out)

    def _L0_ffn_ref(x, ln1_w, ln1_b, ln2_w, ln2_b, conv_w, attn_w, proj_w, router_w, expert_wv, expert_proj):
        import jax, jax.numpy as jnp
        import numpy as np
        EPS = 1e-05

        def _layernorm(x, w, b):
            mu = jnp.mean(x, axis=-1, keepdims=True)
            var = jnp.mean((x - mu) ** 2, axis=-1, keepdims=True)
            return (x - mu) * jax.lax.rsqrt(var + EPS) * w + b

        def _rope_tables(T, D, base=10000.0):
            inv_freq = 1.0 / base ** (jnp.arange(0, D, 2, dtype=jnp.float32) / D)
            t = jnp.arange(T, dtype=jnp.float32)
            freqs = jnp.einsum('i,j->ij', t, inv_freq)
            emb = jnp.concatenate([freqs, freqs], axis=-1)
            return (jnp.cos(emb), jnp.sin(emb))

        def _rotate_half(x):
            x1, x2 = (x[..., :x.shape[-1] // 2], x[..., x.shape[-1] // 2:])
            return jnp.concatenate([-x2, x1], axis=-1)

        def _attn(x, ln_w, ln_b, conv_w, attn_w, proj_w, n_head):
            B, T, C = x.shape
            D = C // n_head
            h = _layernorm(x, ln_w, ln_b)
            hc = jnp.transpose(h, (0, 2, 1))
            hc = jnp.pad(hc, ((0, 0), (0, 0), (2, 0)))
            hc = jax.lax.conv_general_dilated(hc, conv_w, window_strides=(1,), padding='VALID', dimension_numbers=('NCH', 'OIH', 'NCH'), feature_group_count=C)
            h = jnp.transpose(hc, (0, 2, 1))
            qkv = h @ attn_w
            q, k, v = jnp.split(qkv, 3, axis=-1)
            q = q.reshape(B, T, n_head, D)
            k = k.reshape(B, T, n_head, D)
            v = v.reshape(B, T, n_head, D)
            cos, sin = _rope_tables(T, D)
            cos = cos[None, :, None, :]
            sin = sin[None, :, None, :]
            q = q * cos + _rotate_half(q) * sin
            k = k * cos + _rotate_half(k) * sin
            scores = jnp.einsum('bqhd,bkhd->bhqk', q, k) / jnp.sqrt(jnp.float32(D))
            causal = jnp.tril(jnp.ones((T, T), dtype=bool))
            scores = jnp.where(causal, scores, jnp.float32(-1e+30))
            p = jax.nn.softmax(scores, axis=-1)
            y = jnp.einsum('bhqk,bkhd->bqhd', p, v).reshape(B, T, C)
            return y @ proj_w

        def _moe(x, ln_w, ln_b, router_w, expert_wv, expert_proj):
            h = _layernorm(x, ln_w, ln_b)
            logits = h @ router_w
            expert_idx = jnp.argmax(logits, axis=-1)
            E = router_w.shape[-1]
            out = jnp.zeros_like(x)
            for e in range(E):
                gv = h @ expert_wv[e]
                gate_raw, value = jnp.split(gv, 2, axis=-1)
                y = gate_raw * jax.nn.sigmoid(gate_raw) * value @ expert_proj[e]
                out = out + jnp.where((expert_idx == e)[..., None], y, 0.0)
            return out
        n_head = 16
        x = x + _attn(x, ln1_w, ln1_b, conv_w, attn_w, proj_w, n_head)
        x = x + _moe(x, ln2_w, ln2_b, router_w, expert_wv, expert_proj)
        return x
    x = x + _L0_gnn_ref(_layernorm(x, axis=-1), adj, L0_gnn_W_q, L0_gnn_b_q, L0_gnn_W_k, L0_gnn_b_k, L0_gnn_W_v, L0_gnn_b_v)
    x = x + _L0_ffn_ref(_layernorm(x, axis=-1)[None], L0_ffn_ln1_w, L0_ffn_ln1_b, L0_ffn_ln2_w, L0_ffn_ln2_b, L0_ffn_conv_w, L0_ffn_attn_w, L0_ffn_proj_w, L0_ffn_router_w, L0_ffn_expert_wv, L0_ffn_expert_proj)[0]
    return x

_drawn_inputs = setup_inputs


def setup_inputs(seed=0):
    import zlib

    import numpy as np

    out = dict(_drawn_inputs(seed))
    spreads = {'L0_ffn_ln1_w': (1.0, 0.6),
     'L0_ffn_ln1_b': (0.0, 0.8),
     'L0_ffn_ln2_w': (1.0, 0.6),
     'L0_ffn_ln2_b': (0.0, 2.0)}
    factors = {'L0_gnn_b_q': 8.0,
     'L0_gnn_b_k': 64.0,
     'L0_gnn_b_v': 2.995,
     'L0_ffn_conv_w': 8.0,
     'L0_ffn_attn_w': 8.0,
     'L0_ffn_proj_w': 8.0,
     'L0_ffn_router_w': 8.0,
     'L0_ffn_expert_wv': 8.0,
     'L0_ffn_expert_proj': 8.0}
    for name, (base, spread) in spreads.items():
        noise = np.random.default_rng([zlib.crc32(name.encode()), seed]).standard_normal(out[name].shape)
        drawn = base * np.exp(spread * noise) if base else spread * noise
        out[name] = jnp.asarray(drawn.astype(out[name].dtype))
    for name, factor in factors.items():
        out[name] = (out[name] * factor).astype(out[name].dtype)
    return out
```

```python
import numpy as np
from contextlib import ExitStack

import concourse.bass as bass
from concourse import mybir

F32 = mybir.dt.float32
F32R = mybir.dt.float32r
I32 = mybir.dt.int32
U32 = mybir.dt.uint32
ALU = mybir.AluOpType
ACT = mybir.ActivationFunctionType
AX = mybir.AxisListType
ds = bass.ds

P = 128
T = 1354
NT = -(-T // P)
TP = NT * P
TL = T - (NT - 1) * P
D = 512
KB = D // P
EPS = 1e-5
CH = 512

PASSES = ((0, 0), (0, 1), (1, 0))


def f32(ap):
    return ap.bitcast(F32)


def tile_loop(eng, n, step, ahead=0, start=0):
    assert start % 2 == 0
    m = (n - ahead - start) // 2
    if m > 1:
        with eng.Fori(0, m) as i:
            step(2 * i + start, 0, ahead)
            step(2 * i + (start + 1), 1, ahead)
        first = start + 2 * m
    else:
        first = start
    for t in range(first, n):
        step(t, t % 2, n - 1 - t)


def gnn_projections(nc, sem, io, keep):
    with ExitStack() as ctx:
        sb = lambda name, shape, dt=F32: ctx.enter_context(nc.sbuf_tensor(name, shape, dt))
        psum = lambda name, shape: ctx.enter_context(nc.psum_tensor(name, shape, F32))
        qT, kT, v = keep["qT"], keep["kT"], keep["v"]
        ident, minus_half, eps = keep["ident"], keep["minus_half"], keep["eps"]

        GT = CH // P
        groups = [range(g, min(g + GT, NT)) for g in range(0, NT, GT)]
        w_raw = [qT[:, :, c:c + D] for c in (0, D, D)]
        w = [[sb(f"a_w{n}_{part}", [P, KB, D], F32R) for part in ("hi", "lo")] for n in range(3)]
        bq = sb("a_bq", [P, KB])
        bk = sb("a_bk", [P, KB])
        bv = sb("a_bv", [P, D])
        x_in = [sb(f"a_x{b}", [P, D]) for b in range(2)]
        h = sb("a_h", [P, D])
        stats = sb("a_stats", [P, 6])
        mv = [sb(f"a_mv{b}", [P, 2]) for b in range(2)]
        rstd = [sb(f"a_rstd{b}", [P, 1]) for b in range(2)]
        hT = [[sb(f"a_hT{b}_{part}", [P, KB, CH], F32R) for part in ("hi", "lo")] for b in range(2)]
        k_sum = [sb(f"a_k_sum{b}", [P, CH]) for b in range(2)]
        v_sum = sb("a_v_sum", [P, D])

        hT_ps = [psum(f"a_hT_ps{b}", [P, KB, P]) for b in range(2)]
        q_ps = [psum(f"a_q_ps{b}", [P, CH]) for b in range(2)]
        k_ps = [psum(f"a_k_ps{b}", [P, CH]) for b in range(2)]
        v_ps = [psum(f"a_v_ps{b}", [P, D]) for b in range(2)]

        w_loaded = [sem(f"a_w_loaded{n}") for n in range(3)]
        bias_loaded = sem("a_bias_loaded")
        x_loaded = [sem(f"a_x_loaded{b}") for b in range(2)]
        w_hi, w_lo = sem("a_w_hi"), sem("a_w_lo")
        stats_done, mv_done = sem("a_stats_done"), sem("a_mv_done")
        var_done, rstd_done = sem("a_var_done"), sem("a_rstd_done")
        h_done, turned = sem("a_h_done"), sem("a_turned")
        hT_hi, hT_lo = sem("a_hT_hi"), sem("a_hT_lo")
        q_made, k_made, v_made = sem("a_q_made"), sem("a_k_made"), sem("a_v_made")
        q_out, k_summed, v_summed = sem("a_q_out"), sem("a_k_summed"), sem("a_v_summed")
        k_hi, k_lo, v_hi, v_lo = sem("a_k_hi"), sem("a_k_lo"), sem("a_v_hi"), sem("a_v_lo")

        weights = (io["w_q"], io["w_k"], io["w_v"])
        x_tiles = io["x"].rearrange("(t p) d -> t p d", p=P)
        block = ctx.enter_context(nc.Block())

        def place(t):
            return t // GT % 2, (t % GT) * P

        @block.sync
        def _(sp):
            for t in range(NT):
                if t >= 2:
                    sp.wait_ge(h_done, t - 1)
                sp.dma_start(x_in[t % 2][:], x_tiles[t]).then_inc(x_loaded[t % 2], 16)
                if t == 0:
                    sp.dma_start(ident[:], io["ident"]).then_inc(keep["ident_loaded"], 16)
                if t == 1:
                    for n in range(2):
                        sp.dma_start(w_raw[n], weights[n].rearrange("(k p) n -> p k n", p=P)).then_inc(w_loaded[n], 16)
                    sp.dma_start(bq[:], io["b_q"]).then_inc(bias_loaded, 16)
                    sp.dma_start(bk[:], io["b_k"]).then_inc(bias_loaded, 16)
                    sp.dma_start(bv[:], io["b_v"].partition_broadcast(P)).then_inc(bias_loaded, 16)
                if t == 4:
                    sp.wait_ge(w_lo, 2)
                    sp.dma_start(w_raw[2], weights[2].rearrange("(k p) n -> p k n", p=P)).then_inc(w_loaded[2], 16)

        @block.gpsimd
        def _(pool):
            nc.gpsimd.memset(minus_half[:], -0.5).then_inc(keep["const_done"], 1)
            nc.gpsimd.memset(eps[:], EPS).then_inc(keep["const_done"], 1)
            pool.wait_ge(keep["const_done"], 2)

            def inverse_deviation(t):
                b = t % 2
                pool.wait_ge(mv_done, t + 1)
                nc.gpsimd.tensor_tensor(mv[b][:, 1:2], mv[b][:, 1:2], eps[:], ALU.add).then_inc(var_done, 1)
                pool.wait_ge(var_done, t + 1)
                nc.gpsimd.tensor_tensor(rstd[b][:], mv[b][:, 1:2], minus_half[:], ALU.pow).then_inc(rstd_done, 1)

            def k_low(g, o):
                n, c, width = g * KB + o, g * CH, len(groups[g]) * P
                pool.wait_ge(k_hi, n + 1)
                nc.gpsimd.tensor_tensor(kT[1][:, o, c:c + width], k_sum[n % 2][:, 0:width], f32(kT[0][:, o, c:c + width]),
                                        ALU.subtract).then_inc(k_lo, 1)

            def v_low(t):
                pool.wait_ge(v_hi, t + 1)
                nc.gpsimd.tensor_tensor(v[1][:, t, :], v_sum[:], f32(v[0][:, t, :]), ALU.subtract).then_inc(v_lo, 1)

            for t in groups[0]:
                inverse_deviation(t)
            for g, tiles in enumerate(groups):
                following = list(groups[g + 1]) if g + 1 < len(groups) else []
                for t in following:
                    inverse_deviation(t)
                for o in range(KB):
                    k_low(g, o)
                for t in tiles:
                    v_low(t)

        @block.vector
        def _(dve):
            def normalise(t):
                b = t % 2
                dve.wait_ge(x_loaded[b], 16 * (t // 2 + 1))
                nc.vector.bn_stats(stats[:], x_in[b][:]).then_inc(stats_done, 1)
                dve.wait_ge(stats_done, t + 1)
                nc.vector.bn_aggr(mv[b][:], stats[:]).then_inc(mv_done, 1)
                dve.wait_ge(rstd_done, t + 1)
                if t >= 1:
                    dve.wait_ge(turned, t)
                nc.vector.tensor_scalar(h[:], x_in[b][:], mv[b][:, 0:1], rstd[b][:], ALU.subtract, ALU.mult).then_inc(h_done, 1)

            def low_part(t):
                b, c = place(t)
                dve.wait_ge(hT_hi, t + 1)
                nc.vector.tensor_tensor(hT[b][1][:, :, c:c + P], hT_ps[t % 2][:], f32(hT[b][0][:, :, c:c + P]),
                                        ALU.subtract).then_inc(hT_lo, 1)

            def split_weight(n):
                dve.wait_ge(w_hi, n + 1)
                nc.vector.tensor_tensor(w[n][1][:], w_raw[n], f32(w[n][0][:]), ALU.subtract).then_inc(w_lo, 1)

            normalise(0)
            for t in groups[0]:
                if t + 1 in groups[0]:
                    normalise(t + 1)
                low_part(t)
                if t < 2:
                    split_weight(t)
            dve.wait_ge(bias_loaded, 48)
            split_weight(2)

            for g, tiles in enumerate(groups):
                following = list(groups[g + 1]) if g + 1 < len(groups) else []
                width = len(tiles) * P
                if following:
                    normalise(following[0])
                for o in range(KB):
                    if o + 1 < len(following):
                        normalise(following[o + 1])
                    if o < len(following):
                        low_part(following[o])
                    n = g * KB + o
                    dve.wait_ge(k_made, n + 1)
                    if n >= 2:
                        dve.wait_ge(k_lo, n - 1)
                    nc.vector.tensor_scalar(k_sum[n % 2][:, 0:width], k_ps[n % 2][:, 0:width], bk[:, o:o + 1], None,
                                            ALU.add).then_inc(k_summed, 1)
                for t in tiles:
                    dve.wait_ge(v_made, t + 1)
                    if t >= 1:
                        dve.wait_ge(v_lo, t)
                    nc.vector.tensor_tensor(v_sum[:], v_ps[t % 2][:], bv[:], ALU.add).then_inc(v_summed, 1)

        @block.scalar
        def _(act):
            def high_part(t):
                b, c = place(t)
                act.wait_ge(turned, t + 1)
                if t // GT >= 2:
                    act.wait_ge(v_made, (t // GT - 1) * GT)
                nc.scalar.copy(hT[b][0][:, :, c:c + P], hT_ps[t % 2][:]).then_inc(hT_hi, 1)

            def split_weight(n):
                act.wait_ge(w_loaded[n], 16)
                nc.scalar.copy(w[n][0][:], w_raw[n]).then_inc(w_hi, 1)

            for t in groups[0]:
                high_part(t)
                if t < 2:
                    split_weight(t)
            split_weight(2)
            act.wait_ge(bias_loaded, 48)
            act.wait_ge(w_lo, 3)
            for g, tiles in enumerate(groups):
                following = list(groups[g + 1]) if g + 1 < len(groups) else []
                c, width = g * CH, len(tiles) * P
                for o in range(KB):
                    n = g * KB + o
                    act.wait_ge(q_made, n + 1)
                    nc.scalar.activation(qT[:, o, c:c + width], q_ps[n % 2][:, 0:width], ACT.Identity, bias=bq[:, o:o + 1],
                                         scale=1.0).then_inc(q_out, 1)
                for o in range(KB):
                    if o < len(following):
                        high_part(following[o])
                    n = g * KB + o
                    act.wait_ge(k_summed, n + 1)
                    nc.scalar.copy(kT[0][:, o, c:c + width], k_sum[n % 2][:, 0:width]).then_inc(k_hi, 1)
                for t in tiles:
                    act.wait_ge(v_summed, t + 1)
                    nc.scalar.copy(v[0][:, t, :], v_sum[:]).then_inc(v_hi, 1)

        @block.tensor
        def _(pe):
            def turn(t):
                pe.wait_ge(h_done, t + 1)
                if t >= 2:
                    pe.wait_ge(hT_lo, t - 1)
                for k in range(KB):
                    last = nc.tensor.transpose(hT_ps[t % 2][:, k, :], h[:, k * P:(k + 1) * P], ident[:])
                last.then_inc(turned, 1)

            def feature_major(n, o, g, width, out_ps, made, free):
                count = g * KB + o
                if g == 0:
                    pe.wait_ge(w_lo, n + 1)
                if count >= 2:
                    pe.wait_ge(free, count - 1)
                for m, (k, (pw, ph)) in enumerate((k, ps) for k in range(KB) for ps in PASSES):
                    last = nc.tensor.matmul(out_ps[count % 2][:, 0:width], w[n][pw][:, k, o * P:(o + 1) * P],
                                            hT[g % 2][ph][:, k, 0:width], start=(m == 0), stop=(m == 3 * KB - 1))
                last.then_inc(made, 1)

            pe.wait_ge(keep["ident_loaded"], 16)
            for t in groups[0]:
                turn(t)
            for g, tiles in enumerate(groups):
                following = list(groups[g + 1]) if g + 1 < len(groups) else []
                width = len(tiles) * P
                pe.wait_ge(hT_lo, tiles[-1] + 1)
                for o in range(KB):
                    feature_major(0, o, g, width, q_ps, q_made, q_out)
                for o in range(KB):
                    if o < len(following):
                        turn(following[o])
                    feature_major(1, o, g, width, k_ps, k_made, k_summed)
                pe.wait_ge(w_lo, 3)
                for t in tiles:
                    b, c = place(t)
                    if t >= 2:
                        pe.wait_ge(v_summed, t - 1)
                    for m, (k, (ph, pw)) in enumerate((k, ps) for k in range(KB) for ps in PASSES):
                        last = nc.tensor.matmul(v_ps[t % 2][:], hT[b][ph][:, k, c:c + P], w[2][pw][:, k, :],
                                                start=(m == 0), stop=(m == 3 * KB - 1))
                    last.then_inc(v_made, 1)


def graph_attention(nc, sem, io, keep):
    with ExitStack() as ctx:
        sb = lambda name, shape, dt=F32: ctx.enter_context(nc.sbuf_tensor(name, shape, dt))
        psum = lambda name, shape: ctx.enter_context(nc.psum_tensor(name, shape, F32))
        qT, kT, v, ident = keep["qT"], keep["kT"], keep["v"], keep["ident"]

        x1 = [sb(f"b_x1_{b}", [P, D]) for b in range(2)]
        adj = [sb(f"b_adj{b}", [P, T]) for b in range(2)]
        spare = sb("b_spare", [P, T])
        hole = sb("b_hole", [P, T])
        score = sb("b_score", [P, T])
        prob = [sb(f"b_prob{b}", [P, T]) for b in range(2)]
        q = [[sb(f"b_q{b}_{part}", [P, KB, P], F32R) for part in ("hi", "lo")] for b in range(2)]
        pT = [sb(f"b_pT_{part}", [P, NT, P], F32R) for part in ("hi", "lo")]
        top = sb("b_top", [P, 1])
        minus_top = [sb(f"b_minus_top{b}", [P, 1]) for b in range(2)]
        total = [sb(f"b_total{b}", [P, 1]) for b in range(2)]
        inv_total = [sb(f"b_inv_total{b}", [P, 1]) for b in range(2)]
        o = [sb(f"b_o{b}", [P, D]) for b in range(2)]
        moments = sb("b_moments", [P, 6])
        mv = [sb(f"b_mv{n}", [P, 2]) for n in range(2)]
        rstd = [sb(f"b_rstd{n}", [P, 1]) for n in range(2)]
        spacer = sb("b_spacer", [P, 1])
        normed = [[sb(f"b_normed{n}_{b}", [P, D]) for b in range(2)] for n in range(2)]

        s_ps = psum("b_s_ps", [P, 3 * CH])
        pT_ps = psum("b_pT_ps", [P, 12, P])
        o_ps = psum("b_o_ps", [P, D])

        x_loaded = [sem(f"b_x_loaded{b}") for b in range(2)]
        adj_loaded = [sem(f"b_adj_loaded{b}") for b in range(2)]
        q_hi = sem("b_q_hi")
        q_lo = sem("b_q_lo")
        s_made = sem("b_s_made")
        spare_done = sem("b_spare_done")
        hole_done = sem("b_hole_done")
        score_done = sem("b_score_done")
        minus_top_done = sem("b_minus_top_done")
        prob_done = sem("b_prob_done")
        inv_total_done = sem("b_inv_total_done")
        p_turned = sem("b_p_turned")
        pT_hi = sem("b_pT_hi")
        pT_lo = sem("b_pT_lo")
        o_made = sem("b_o_made")
        o_done = sem("b_o_done")
        x1_done = sem("b_x1_done")
        moments_done = [sem(f"b_moments_done{n}") for n in range(2)]
        mv_done = [sem(f"b_mv_done{n}") for n in range(2)]
        var_done = [sem(f"b_var_done{n}") for n in range(2)]
        rstd_done = [sem(f"b_rstd_done{n}") for n in range(2)]
        normed_done = [sem(f"b_normed_done{n}") for n in range(2)]
        stored = [sem(f"b_stored{b}") for b in range(2)]

        SCALE = D ** -0.5

        def rounds(eng, step):
            for i in range(4):
                step(i, i % 2)
            with eng.Fori(2, (NT - 1) // 2) as j:
                step(2 * j, 0)
                step(2 * j + 1, 1)
            for i in range(NT - 1, NT + 3):
                step(i, i % 2)

        def has(i, lag):
            return not isinstance(i, int) or 0 <= i - lag < NT

        block = ctx.enter_context(nc.Block())

        @block.sync
        def _(sp):
            for b in range(2):
                sp.dma_start(adj[b][:], io["adj"][b * P:(b + 1) * P, :]).then_inc(adj_loaded[b], 16)
            for b in range(2):
                sp.dma_start(x1[b][:], io["x"][b * P:(b + 1) * P, :]).then_inc(x_loaded[b], 16)
            for k, tile in enumerate(keep["attn_w_raw"]):
                sp.dma_start(tile[:], io["attn_w"][k * P:(k + 1) * P, :]).then_inc(keep["attn_w_loaded"][k], 16)

            def step(i, b):
                if has(i, -1) and not (isinstance(i, int) and i == 0):
                    sp.wait_ge(spare_done, i)
                    sp.dma_start(adj[1 - b][:], io["adj"][ds((i + 1) * P, P), :]).then_inc(adj_loaded[1 - b], 16)
                if has(i, 3):
                    for what, tile, done in (("x1", x1[1 - b][:], x1_done), ("t", normed[0][1 - b][:], normed_done[0]),
                                             ("g", normed[1][1 - b][:], normed_done[1])):
                        sp.wait_ge(done, i - 2)
                        sp.dma_start(keep["dram"][what][ds((i - 3) * P, P), :], tile).then_inc(stored[1 - b], 16)
                    if has(i, 1):
                        sp.wait_ge(stored[1 - b], 48 * ((i - 3) // 2 + 1) if isinstance(i, int) else 24 * i - (24 if b else 48))
                        sp.dma_start(x1[1 - b][:], io["x"][ds((i - 1) * P, P), :]).then_inc(x_loaded[1 - b], 16)
            rounds(sp, step)
            for b in range(2):
                sp.wait_ge(stored[b], 48 * ((NT + 1 - b) // 2))

        @block.tensor
        def _(pe):
            def step(i, b):
                if has(i, 0):
                    pe.wait_ge(q_lo, i + 1)
                    pe.wait_ge(spare_done, i)
                    for c in range(0, T, CH):
                        width = min(CH, T - c)
                        for m, (k, (pq, pk)) in enumerate((k, ps) for k in range(KB) for ps in PASSES):
                            last = nc.tensor.matmul(s_ps[:, c:c + width], q[b][pq][:, k, :], kT[pk][:, k, c:c + width],
                                                    start=(m == 0), stop=(m == 3 * KB - 1))
                    last.then_inc(s_made, 1)
                if has(i, 2):
                    pe.wait_ge(pT_lo, i - 1)
                    pe.wait_ge(pT_hi, i - 1)
                    pe.wait_ge(o_done, i - 2)
                    for j in range(NT):
                        rows = P if j < NT - 1 else TL
                        for m, (pp, pv) in enumerate(PASSES):
                            last = nc.tensor.matmul(o_ps[:], pT[pp][0:rows, j, :], v[pv][0:rows, j, :],
                                                    start=(j == 0 and m == 0), stop=(j == NT - 1 and m == 2))
                    last.then_inc(o_made, 1)
                if has(i, 1):
                    pe.wait_ge(prob_done, i)
                    pe.wait_ge(pT_lo, i - 1)
                    for j in range(NT):
                        cols = P if j < NT - 1 else TL
                        last = nc.tensor.transpose(pT_ps[0:cols, j, :], prob[1 - b][:, j * P:j * P + cols], ident[:])
                    last.then_inc(p_turned, 1)
            rounds(pe, step)

        @block.vector
        def _(dve):
            nc.vector.memset(pT_ps[64:P, NT - 1, :], 0.0).then_inc(keep["pad_cleared"], 1)
            def step(i, b):
                if has(i, 0):
                    dve.wait_ge(s_made, i + 1)
                    dve.wait_ge(adj_loaded[b], 16 * (i // 2 + 1) if isinstance(i, int) else 8 * i + (16 - 8 * b))
                    nc.vector.scalar_tensor_tensor(spare[:], s_ps[:, 0:T], SCALE, adj[b][:], ALU.mult, ALU.mult).then_inc(spare_done, 1)
                    dve.wait_ge(spare_done, i + 1)
                    nc.vector.tensor_scalar(hole[:], spare[:], 0.0, -10000.0, ALU.is_equal, ALU.mult).then_inc(hole_done, 1)
                    dve.wait_ge(hole_done, i + 1)
                    dve.wait_ge(prob_done, i)
                if has(i, 1):
                    dve.wait_ge(prob_done, i)
                    if not isinstance(i, int) or i >= 3:
                        dve.wait_ge(o_done, i - 2)
                    nc.vector.reciprocal(inv_total[1 - b][:], total[1 - b][:]).then_inc(inv_total_done, 1)
                if has(i, 0):
                    nc.vector.tensor_tensor_reduce(score[:], spare[:], hole[:], 1.0, -3.0e38, ALU.add, ALU.max,
                                                   top[:]).then_inc(score_done, 1)
                    dve.wait_ge(score_done, i + 1)
                    nc.vector.tensor_scalar(minus_top[b][:], top[:], -1.0, None, ALU.mult).then_inc(minus_top_done, 1)
                if has(i, 1):
                    dve.wait_ge(p_turned, i)
                    dve.wait_ge(pT_hi, i)
                    if not isinstance(i, int) or i >= 2:
                        dve.wait_ge(o_made, i - 1)
                    nc.vector.tensor_tensor(pT[1][:], pT_ps[:, 0:NT, :], f32(pT[0][:]), ALU.subtract).then_inc(pT_lo, 1)
                if has(i, 3):
                    for n in range(2):
                        if n == 0:
                            dve.wait_ge(x1_done, i - 2)
                            nc.vector.bn_stats(moments[:], x1[1 - b][:]).then_inc(moments_done[n], 1)
                        else:
                            dve.wait_ge(normed_done[0], i - 2)
                            nc.vector.bn_stats(moments[:], normed[0][1 - b][:]).then_inc(moments_done[n], 1)
                        dve.wait_ge(moments_done[n], i - 2)
                        nc.vector.memset(spacer[:], 0.0)
                        nc.vector.bn_aggr(mv[n][:], moments[:]).then_inc(mv_done[n], 1)
                        dve.wait_ge(mv_done[n], i - 2)
                        dve.wait_ge(rstd_done[n], i - 2)
                        if not isinstance(i, int):
                            dve.wait_ge(stored[1 - b], 24 * i - (96 if b == 0 else 72))
                        elif i >= 5:
                            dve.wait_ge(stored[1 - b], 48 * ((i - 3) // 2))
                        source = x1[1 - b][:] if n == 0 else normed[0][1 - b][:]
                        nc.vector.tensor_scalar(normed[n][1 - b][:], source, mv[n][:, 0:1], rstd[n][:],
                                                ALU.subtract, ALU.mult).then_inc(normed_done[n], 1)
            rounds(dve, step)

        @block.scalar
        def _(act):
            def split_q(t, b):
                if not (isinstance(t, int) and t < 2):
                    act.wait_ge(s_made, t - 1)
                nc.scalar.copy(q[b][0][:], qT[:, :, ds(t * P, P)]).then_inc(q_hi, 1)

            split_q(0, 0)
            act.wait_ge(keep["pad_cleared"], 1)

            def step(i, b):
                if has(i, -1):
                    split_q(i + 1, 1 - b)
                if has(i, 0):
                    act.wait_ge(minus_top_done, i + 1)
                    if has(i, 2):
                        act.wait_ge(p_turned, i - 1)
                        act.wait_ge(inv_total_done, i - 1)
                    nc.scalar.activation(prob[b][:], score[:], ACT.Exp, bias=minus_top[b][:], scale=1.0,
                                         accum_out=total[b][:]).then_inc(prob_done, 1)
                if has(i, 2):
                    act.wait_ge(o_made, i - 1)
                    act.wait_ge(inv_total_done, i - 1)
                    if has(i, 4):
                        act.wait_ge(x1_done, i - 3)
                    nc.scalar.activation(o[b][:], o_ps[:], ACT.Relu, scale=inv_total[b][:]).then_inc(o_done, 1)
                if has(i, 1):
                    act.wait_ge(p_turned, i)
                    if not isinstance(i, int) or i >= 2:
                        act.wait_ge(o_made, i - 1)
                    nc.scalar.copy(pT[0][:], pT_ps[:, 0:NT, :]).then_inc(pT_hi, 1)
            rounds(act, step)

        @block.gpsimd
        def _(pool):
            def split_q(t, b):
                pool.wait_ge(q_hi, t + 1)
                nc.gpsimd.tensor_tensor(q[b][1][:], qT[:, :, ds(t * P, P)], f32(q[b][0][:]), ALU.subtract).then_inc(q_lo, 1)

            split_q(0, 0)

            def step(i, b):
                if has(i, -1):
                    split_q(i + 1, 1 - b)
                if has(i, 3):
                    for n in range(2):
                        pool.wait_ge(mv_done[n], i - 2)
                        nc.gpsimd.tensor_tensor(mv[n][:, 1:2], mv[n][:, 1:2], keep["eps"][:], ALU.add).then_inc(var_done[n], 1)
                        pool.wait_ge(var_done[n], i - 2)
                        nc.gpsimd.tensor_tensor(rstd[n][:], mv[n][:, 1:2], keep["minus_half"][:], ALU.pow).then_inc(rstd_done[n], 1)
                if has(i, 2):
                    pool.wait_ge(o_done, i - 1)
                    pool.wait_ge(x_loaded[b], 16 * (i // 2) if isinstance(i, int) else 8 * i - 8 * b)
                    nc.gpsimd.tensor_tensor(x1[b][:], x1[b][:], o[b][:], ALU.add).then_inc(x1_done, 1)
            rounds(pool, step)


H = 16
HD = D // H
HV = HD + 1


def ffn_projections(nc, sem, io, keep):
    with ExitStack() as ctx:
        sb = lambda name, shape, dt=F32: ctx.enter_context(nc.sbuf_tensor(name, shape, dt))
        psum = lambda name, shape: ctx.enter_context(nc.psum_tensor(name, shape, F32))
        qk, vv, ident = keep["qk"], keep["vv"], keep["ident"]
        N3 = 3 * D

        w_raw = keep["attn_w_raw"] + [sb("c_w_raw", [P, N3])]
        w = [sb(f"c_w_{part}", [P, KB, N3], F32R) for part in ("hi", "lo")]
        ln_w, ln_b = sb("c_ln_w", [P, KB]), sb("c_ln_b", [P, KB])
        taps = sb("c_taps", [P, KB, 3])
        rope = sb("c_rope", [P, 2, NT, HD])
        g_in = [sb(f"c_g{b}", [P, D]) for b in range(2)]
        hT = [sb(f"c_hT{b}", [P, KB, P + 2]) for b in range(2)]
        part_sum = [sb(f"c_part_sum{n}", [P, KB, P]) for n in range(2)]
        conv = sb("c_conv", [P, KB, P])
        convT = [[sb(f"c_convT{b}_{part}", [P, KB, P], F32R) for part in ("hi", "lo")] for b in range(2)]
        by_cos = sb("c_by_cos", [P, 2 * H, HD])
        by_sin = sb("c_by_sin", [P, 2 * H, HD])

        hT_ps = [psum(f"c_hT_ps{b}", [P, KB, P]) for b in range(2)]
        qkv_ps = [psum(f"c_qkv_ps{b}", [P, N3]) for b in range(2)]

        w_loaded = keep["attn_w_loaded"]
        small_loaded = sem("c_small_loaded")
        g_loaded = [sem(f"c_g_loaded{b}") for b in range(2)]
        w_hi, w_lo = sem("c_w_hi"), sem("c_w_lo")
        edge_done, ones_done = sem("c_edge_done"), sem("c_ones_done")
        turned, affine_done, halo_done = sem("c_turned"), sem("c_affine_done"), sem("c_halo_done")
        tap_done, conv_done = [sem(f"c_tap_done{n}") for n in range(2)], sem("c_conv_done")
        conv_hi, conv_lo = sem("c_conv_hi"), sem("c_conv_lo")
        qkv_made, cos_done, sin_done = sem("c_qkv_made"), sem("c_cos_done"), sem("c_sin_done")
        rotated, v_out = sem("c_rotated"), sem("c_v_out")

        block = ctx.enter_context(nc.Block())

        @block.sync
        def _(sp):
            for b in range(2):
                sp.dma_start(g_in[b][:], keep["dram"]["g"][b * P:(b + 1) * P, :]).then_inc(g_loaded[b], 16)
            for tile, name in ((ln_w, "ln1_w"), (ln_b, "ln1_b"), (taps, "conv_w")):
                sp.dma_start(tile[:], io[name]).then_inc(small_loaded, 16)
            sp.dma_start(w_raw[KB - 1][:], io["attn_w"][(KB - 1) * P:KB * P, :]).then_inc(w_loaded[KB - 1], 16)
            sp.dma_start(rope[:], io["rope"]).then_inc(keep["rope_loaded"], 16)

            def step(t, b, _ahead):
                sp.wait_ge(turned, t + 1)
                sp.dma_start(g_in[b][:], keep["dram"]["g"][ds((t + 2) * P, P), :]).then_inc(g_loaded[b], 16)
            tile_loop(sp, NT - 2, step)

        @block.tensor
        def _(pe):
            def turn(t, b):
                pe.wait_ge(g_loaded[b], 16 * (t // 2 + 1) if isinstance(t, int) else 8 * t + (16 - 8 * b))
                if not (isinstance(t, int) and t < 2):
                    pe.wait_ge(affine_done, t - 1)
                for k in range(KB):
                    last = nc.tensor.transpose(hT_ps[b][:, k, :], g_in[b][:, k * P:(k + 1) * P], ident[:])
                last.then_inc(turned, 1)

            turn(0, 0)
            turn(1, 1)
            pe.wait_ge(w_lo, KB)

            def step(t, b, ahead):
                if ahead >= 2:
                    turn(t + 2, b)
                pe.wait_ge(conv_lo, t + 1)
                if not (isinstance(t, int) and t < 2):
                    pe.wait_ge(sin_done, t - 1)
                    pe.wait_ge(v_out, t - 1)
                for c in range(3):
                    for m, (k, (pc, pw)) in enumerate((k, ps) for k in range(KB) for ps in PASSES):
                        last = nc.tensor.matmul(qkv_ps[b][:, c * CH:(c + 1) * CH], convT[b][pc][:, k, :],
                                                w[pw][:, k, c * CH:(c + 1) * CH], start=(m == 0), stop=(m == 3 * KB - 1))
                last.then_inc(qkv_made, 1)
            step(0, 0, 2)
            step(1, 1, 2)
            tile_loop(pe, NT, step, ahead=2, start=2)

        @block.scalar
        def _(act):
            def affine(t, b):
                act.wait_ge(turned, t + 1)
                if not (isinstance(t, int) and t < 2):
                    act.wait_ge(conv_done, t - 1)
                for k in range(KB):
                    last = nc.scalar.activation(hT[b][:, k, 2:], hT_ps[b][:, k, :], ACT.Identity, bias=ln_b[:, k:k + 1],
                                                scale=ln_w[:, k:k + 1])
                last.then_inc(affine_done, 1)

            def halo(t, b):
                act.wait_ge(affine_done, t + 1)
                if not (isinstance(t, int) and t < 1):
                    act.wait_ge(conv_done, t)
                nc.scalar.copy(hT[1 - b][:, :, 0:2], hT[b][:, :, P:P + 2]).then_inc(halo_done, 1)

            def high_part(t, b):
                act.wait_ge(conv_done, t + 1)
                if not (isinstance(t, int) and t < 2):
                    act.wait_ge(qkv_made, t - 1)
                nc.scalar.copy(convT[b][0][:], conv[:]).then_inc(conv_hi, 1)

            def weight_high(k):
                act.wait_ge(w_loaded[k], 16)
                nc.scalar.copy(w[0][:, k, :], w_raw[k][:]).then_inc(w_hi, 1)

            weight_high(0)
            weight_high(1)
            act.wait_ge(small_loaded, 48)
            affine(0, 0)
            halo(0, 0)
            affine(1, 1)
            weight_high(2)
            high_part(0, 0)
            weight_high(3)

            def step(t, b, ahead):
                if ahead >= 2:
                    halo(t + 1, 1 - b)
                    affine(t + 2, b)
                if ahead >= 1:
                    high_part(t + 1, 1 - b)
                act.wait_ge(qkv_made, t + 1)
                nc.scalar.copy(vv[:, ds(t, 1), :, 0:HD], qkv_ps[b][:, 2 * D:3 * D].rearrange("p (a h d) -> p a h d", a=1, h=H)).then_inc(v_out, 1)
            step(0, 0, 2)
            step(1, 1, 2)
            tile_loop(act, NT, step, ahead=2, start=2)

        @block.vector
        def _(dve):
            def convolve(t, b):
                dve.wait_ge(affine_done, t + 1)
                if not (isinstance(t, int) and t == 0):
                    dve.wait_ge(halo_done, t)
                    dve.wait_ge(conv_lo, t)
                for k in range(KB):
                    last = nc.vector.tensor_scalar(part_sum[0][:, k, :], hT[b][:, k, 2:P + 2], taps[:, k, 2:3], None, ALU.mult)
                last.then_inc(tap_done[0], 1)
                dve.wait_ge(tap_done[0], t + 1)
                for k in range(KB):
                    last = nc.vector.scalar_tensor_tensor(part_sum[1][:, k, :], hT[b][:, k, 1:P + 1], taps[:, k, 1:2],
                                                          part_sum[0][:, k, :], ALU.mult, ALU.add)
                last.then_inc(tap_done[1], 1)
                dve.wait_ge(tap_done[1], t + 1)
                for k in range(KB):
                    last = nc.vector.scalar_tensor_tensor(conv[:, k, :], hT[b][:, k, 0:P], taps[:, k, 0:1],
                                                          part_sum[1][:, k, :], ALU.mult, ALU.add)
                last.then_inc(conv_done, 1)

            nc.vector.memset(hT[0][:, :, 0:2], 0.0).then_inc(edge_done, 1)
            nc.vector.memset(vv[:, :, :, HD:HV], 1.0).then_inc(ones_done, 1)
            dve.wait_ge(edge_done, 1)

            def weight_low(k):
                dve.wait_ge(w_hi, k + 1)
                nc.vector.tensor_tensor(w[1][:, k, :], w_raw[k][:], f32(w[0][:, k, :]), ALU.subtract).then_inc(w_lo, 1)

            weight_low(0)
            weight_low(1)
            dve.wait_ge(small_loaded, 48)
            convolve(0, 0)
            weight_low(2)
            weight_low(3)
            dve.wait_ge(keep["rope_loaded"], 16)

            def step(t, b, ahead):
                if ahead >= 1:
                    convolve(t + 1, 1 - b)
                dve.wait_ge(qkv_made, t + 1)
                dve.wait_ge(rotated, t)
                x = qkv_ps[b][:, 0:2 * D].rearrange("p (h d) -> p h d", d=HD)
                cos, sin = (rope[:, n, ds(t, 1), :].to_broadcast([P, 2 * H, HD]) for n in range(2))
                half = HD // 2
                nc.vector.tensor_tensor(by_cos[:], x, cos, ALU.mult).then_inc(cos_done, 1)
                nc.vector.tensor_tensor(by_sin[:, :, 0:half], x[:, :, half:HD], sin[:, :, 0:half], ALU.mult)
                nc.vector.tensor_tensor(by_sin[:, :, half:HD], x[:, :, 0:half], sin[:, :, half:HD], ALU.mult).then_inc(sin_done, 1)
            step(0, 0, 2)
            step(1, 1, 2)
            tile_loop(dve, NT, step, ahead=2, start=2)

        @block.gpsimd
        def _(pool):
            def low_part(t, b):
                pool.wait_ge(conv_hi, t + 1)
                nc.gpsimd.tensor_tensor(convT[b][1][:], conv[:], f32(convT[b][0][:]), ALU.subtract).then_inc(conv_lo, 1)

            low_part(0, 0)

            def step(t, b, ahead):
                if ahead >= 1:
                    low_part(t + 1, 1 - b)
                pool.wait_ge(cos_done, t + 1)
                pool.wait_ge(sin_done, t + 1)
                nc.gpsimd.tensor_tensor(qk[:, ds(t, 1), :], by_cos[:].rearrange("p (a h) d -> p a (h d)", a=1),
                                        by_sin[:].rearrange("p (a h) d -> p a (h d)", a=1), ALU.add).then_inc(rotated, 1)
            tile_loop(pool, NT, step, ahead=2)


def block_chunks(blocks):
    width = blocks * P
    if blocks in (5, 9):
        banks = -(-width // CH)
        return [(CH * n, width // banks * n, width // banks) for n in range(banks)]
    return [(c, c, min(CH, width - c)) for c in range(0, width, CH)]


def row_view(ps, blocks):
    chunks = block_chunks(blocks)
    if blocks in (5, 9):
        return ps[:, 0:len(chunks) * CH].rearrange("p (n c) -> p n c", c=CH)[:, :, 0:chunks[0][2]]
    return ps[:, 0:blocks * P]


def row_split(ap, blocks):
    if blocks in (5, 9):
        return ap.rearrange("p (n c) -> p n c", n=len(block_chunks(blocks)))
    return ap


def causal_attention(nc, sem, io, keep):
    with ExitStack() as ctx:
        sb = lambda name, shape, dt=F32: ctx.enter_context(nc.sbuf_tensor(name, shape, dt))
        psum = lambda name, shape: ctx.enter_context(nc.psum_tensor(name, shape, F32))
        qk, vv, ident, y = keep["qk"], keep["vv"], keep["ident"], keep["y"]
        BF16 = mybir.dt.bfloat16

        zeros = sb("d_zeros", [P, D])
        later = sb("d_later", [P, 2, P])
        later_bf = sb("d_later_bf", [P, 2, P], BF16)
        ident_bf = sb("d_ident_bf", [P, P], BF16)
        q_stack = sb("d_q_stack", [P, NT, P], F32R)
        k_stack = sb("d_k_stack", [P, NT, P], F32R)
        qT = [sb(f"d_qT{b}", [P, TP], F32R) for b in range(2)]
        kT = [sb(f"d_kT{b}", [P, TP], F32R) for b in range(2)]
        start_of = [sum(NT - m for m in range(j)) * P for j in range(NT + 1)]
        probs = [sb(f"d_probs{b}", [P, start_of[NT]]) for b in range(2)]
        v_head = [sb(f"d_v_head{b}", [P, NT, HV]) for b in range(2)]
        top = sb("d_top", [P, NT])
        minus_top = sb("d_minus_top", [P, 2 * NT], F32R)
        minus_topT = sb("d_minus_topT", [2 * NT, P], F32R)
        inv_total = sb("d_inv_total", [P, NT])

        s2_ps = psum("d_s2_ps", [P, 3 * CH])
        s1_ps = psum("d_s1_ps", [P, 3 * CH])
        o_ps = [psum(f"d_o_ps{b}", [P, CH]) for b in range(2)]
        both_ps = (s1_ps, s2_ps)
        MT = 3 * P

        zeros_done, cleared = sem("d_zeros_done"), sem("d_cleared")
        mask_loaded, masks_done, pads_done = sem("d_mask_loaded"), sem("d_masks_done"), sem("d_pads_done")
        q_hi, q_lo, k_hi, k_lo = sem("d_q_hi"), sem("d_q_lo"), sem("d_k_hi"), sem("d_k_lo")
        v_ready = sem("d_v_ready")
        q_turned, k_turned, qT_out, kT_out = sem("d_q_turned"), sem("d_k_turned"), sem("d_qT_out"), sem("d_kT_out")
        s1_made, top_done, s2_made, exp_done = sem("d_s1_made"), sem("d_top_done"), sem("d_s2_made"), sem("d_exp_done")
        top_hi, top_split, top_turned, top_out, top_placed = (sem(f"d_top_{x}") for x in ("hi", "split", "turned", "out", "placed"))
        o_made, inv_done, y_done = sem("d_o_made"), sem("d_inv_done"), sem("d_y_done")

        SCALE = HD ** -0.5

        def has(h, lag):
            return not isinstance(h, int) or 0 <= h - lag < H

        def rounds(eng, step):
            for h in (0, 1):
                step(h, h % 2)
            with eng.Fori(1, H // 2 - 1) as j:
                step(2 * j, 0)
                step(2 * j + 1, 1)
            for h in range(H - 2, H + 2):
                step(h, h % 2)

        def beyond(h, n):
            return not isinstance(h, int) or h >= n

        block = ctx.enter_context(nc.Block())

        @block.tensor
        def _(pe):
            def turn(which, g, b, stack, low, turned):
                ps = s2_ps if which == "q" else s1_ps
                pe.wait_ge(low, g + 1)
                for t in range(NT):
                    last = nc.tensor.transpose(ps[:, t * P:(t + 1) * P], f32(stack[:, t, :]), ident[:])
                last.then_inc(turned, 1)

            def token_major(g, b, j, ps=s1_ps):
                i = NT - 1 - j
                chunks = block_chunks(i + 1)
                for n, (at, c, width) in enumerate(chunks):
                    final = n == len(chunks) - 1
                    last = nc.tensor.matmul(ps[:, at:at + width], qT[b][:, i * P:(i + 1) * P], kT[b][:, c:c + width],
                                            start=True, stop=not final)
                last = nc.tensor.matmul(ps[:, at + width - P:at + width], ident_bf[:], later_bf[:, 0, :], start=False, stop=True)
                last.then_inc(s1_made, 1)

            def key_major(b, j):
                for n, (at, c, width) in enumerate(block_chunks(NT - j)):
                    last = nc.tensor.matmul(s2_ps[:, at:at + width], kT[b][:, j * P:(j + 1) * P],
                                            qT[b][:, j * P + c:j * P + c + width], start=True, stop=n > 0)
                    if n == 0:
                        last = nc.tensor.matmul(s2_ps[:, at:at + P], ident_bf[:], later_bf[:, 1, :], start=False, stop=True)
                last.then_inc(s2_made, 1)

            products = [(i, j) for i in range(NT - 1, -1, -1) for j in range(i + 1)]
            SHARES = (4, 6, 6, 6, 6, 6, 5, 5, 4, 4, 4, 4, 6)
            assert sum(SHARES) == len(products) and len(SHARES) == NT + 2

            def product(b, i, j):
                c = start_of[j] + (i - j) * P
                return nc.tensor.matmul(o_ps[b][:, i * HV:(i + 1) * HV], probs[b][:, c:c + P], v_head[b][:, j, :],
                                        start=(j == 0), stop=(j == i))

            def times_v(h, b, n):
                if n == 0:
                    pe.wait_ge(v_ready, h + 1)
                    pe.wait_ge(exp_done, NT * (h + 1))
                    if beyond(h, 2):
                        pe.wait_ge(y_done, h - 1)
                first = sum(SHARES[:n])
                for i, j in products[first:first + SHARES[n]]:
                    last = product(b, i, j)
                if n == len(SHARES) - 1:
                    last.then_inc(o_made, 1)

            def tile_times_v(b, i):
                if i == 0:
                    pe.wait_ge(v_ready, H)
                    pe.wait_ge(y_done, H - 2)
                for j in range(i + 1):
                    last = product(b, i, j)
                if i == NT - 1:
                    last.then_inc(o_made, 1)

            def turn_top(g, b):
                pe.wait_ge(top_split, g + 1)
                if beyond(g, 1):
                    pe.wait_ge(top_out, g)
                nc.tensor.transpose(o_ps[b][0:2 * NT, MT:MT + P], f32(minus_top[:]), ident[:]).then_inc(top_turned, 1)

            pe.wait_ge(masks_done, 2)
            pe.wait_ge(pads_done, 3)
            turn("q", 0, 0, q_stack, q_lo, q_turned)
            turn("k", 0, 0, k_stack, k_lo, k_turned)
            pe.wait_ge(qT_out, 1)
            pe.wait_ge(kT_out, 1)
            for j in range(NT):
                if j >= 2:
                    pe.wait_ge(top_done, j - 1)
                token_major(0, 0, j, ps=both_ps[j % 2])
            pe.wait_ge(top_done, NT - 1)
            turn("q", 1, 1, q_stack, q_lo, q_turned)
            turn_top(0, 1)
            pe.wait_ge(top_done, NT)
            turn("k", 1, 1, k_stack, k_lo, k_turned)

            def step(h, b):
                last_head = isinstance(h, int) and h == H - 1
                behind = has(h, 1) and has(h, 0)
                if has(h, 0):
                    pe.wait_ge(top_placed, 32 * (h + 1))
                if has(h, -1):
                    pe.wait_ge(qT_out, h + 2)
                for j in range(NT):
                    if has(h, 0):
                        if not (isinstance(h, int) and h == 0 and j == 0):
                            pe.wait_ge(exp_done, NT * h + j)
                        key_major(b, j)
                    if behind and j < 11:
                        times_v(h - 1, 1 - b, j)
                    if has(h, -1):
                        if j == 0:
                            pe.wait_ge(kT_out, h + 2)
                        pe.wait_ge(top_done, NT * (h + 1) + j)
                        token_major(h + 1, 1 - b, j)
                    if behind and j >= 11:
                        times_v(h - 1, 1 - b, j)
                    if last_head and j > 0:
                        tile_times_v(b, j - 1)
                if behind:
                    times_v(h - 1, 1 - b, NT)
                if has(h, -1):
                    turn_top(h + 1, b)
                if has(h, -2):
                    pe.wait_ge(exp_done, NT * (h + 1))
                    turn("q", h + 2, b, q_stack, q_lo, q_turned)
                    pe.wait_ge(top_done, NT * (h + 2))
                    turn("k", h + 2, b, k_stack, k_lo, k_turned)
                if behind:
                    times_v(h - 1, 1 - b, NT + 1)
                if last_head:
                    pe.wait_ge(exp_done, NT * H)
                    tile_times_v(b, NT - 1)
            rounds(pe, step)

        @block.scalar
        def _(act):
            def stack_high(g, b):
                if beyond(g, 1):
                    act.wait_ge(q_turned, g)
                    act.wait_ge(k_turned, g)
                nc.scalar.copy(q_stack[:, :, 0:2 * HD].rearrange("p t (c d) -> p t c d", c=2),
                               qk[:, :, ds(g * HD, HD)].unsqueeze(2).to_broadcast([P, NT, 2, HD])).then_inc(q_hi, 1)
                nc.scalar.copy(k_stack[:].rearrange("p t (c d) -> p t c d", c=2)[:, :, :, 0:HD],
                               qk[:, :, ds(g * HD + D, HD)].unsqueeze(2).to_broadcast([P, NT, 2, HD])).then_inc(k_hi, 1)

            def qT_copy(g, b):
                act.wait_ge(q_turned, g + 1)
                if beyond(g, 2):
                    act.wait_ge(s2_made, NT * (g - 1))
                nc.scalar.copy(qT[b][:], s2_ps[:, 0:TP]).then_inc(qT_out, 1)

            act.wait_ge(pads_done, 3)
            stack_high(0, 0)
            qT_copy(0, 0)
            stack_high(1, 1)
            qT_copy(1, 1)

            def step(h, b):
                for j in range(NT):
                    if has(h, 0):
                        act.wait_ge(s2_made, NT * h + j + 1)
                        if j == 0 and beyond(h, 2):
                            act.wait_ge(o_made, h - 1)
                        row = probs[b][:, start_of[j]:start_of[j + 1]]
                        nc.scalar.activation(row_split(row, NT - j), row_view(s2_ps, NT - j), ACT.Exp, scale=SCALE).then_inc(exp_done, 1)
                    if j == 3 and has(h, -2):
                        stack_high(h + 2, b)
                if has(h, -2):
                    qT_copy(h + 2, b)
            rounds(act, step)

        @block.vector
        def _(dve):
            def kT_copy(g, b):
                dve.wait_ge(k_turned, g + 1)
                if beyond(g, 2):
                    dve.wait_ge(s2_made, NT * (g - 1))
                nc.vector.tensor_copy(kT[b][:], s1_ps[:, 0:TP]).then_inc(kT_out, 1)

            def row_top(g, j, ps=s1_ps):
                i = NT - 1 - j
                dve.wait_ge(s1_made, NT * g + j + 1)
                if j == 0 and beyond(g, 1):
                    dve.wait_ge(top_split, g)
                view = row_view(ps, i + 1)
                nc.vector.tensor_reduce(top[:, i:i + 1], view, AX.XY if len(view.shape) == 3 else AX.X, ALU.max).then_inc(top_done, 1)

            def split_top(g):
                dve.wait_ge(top_done, NT * (g + 1))
                if beyond(g, 1):
                    dve.wait_ge(top_turned, g)
                nc.vector.tensor_scalar(minus_top[:, 0:NT], top[:], -1.0, None, ALU.mult).then_inc(top_hi, 1)
                dve.wait_ge(top_hi, g + 1)
                nc.vector.scalar_tensor_tensor(minus_top[:, NT:2 * NT], top[:], -1.0, f32(minus_top[:, 0:NT]), ALU.mult,
                                               ALU.subtract).then_inc(top_split, 1)

            def top_copy(g, b):
                dve.wait_ge(top_turned, g + 1)
                if beyond(g, 1):
                    dve.wait_ge(top_placed, 32 * g)
                nc.vector.tensor_copy(minus_topT[:], o_ps[b][0:2 * NT, MT:MT + P]).then_inc(top_out, 1)

            def y_copy(g, b):
                dve.wait_ge(o_made, g + 1)
                if beyond(g, 1):
                    dve.wait_ge(y_done, g)
                o = o_ps[b][:, 0:NT * HV].rearrange("p (t e) -> p t e", e=HV)
                nc.vector.reciprocal(inv_total[:].unsqueeze(2), o[:, :, HD:HV]).then_inc(inv_done, 1)
                dve.wait_ge(inv_done, g + 1)
                nc.vector.tensor_tensor(y[:, :, ds(g * HD, HD)], o[:, :, 0:HD], inv_total[:].unsqueeze(2).to_broadcast([P, NT, HD]),
                                        ALU.mult).then_inc(y_done, 1)

            nc.vector.memset(f32(q_stack[:, :, 3 * HD:P]), 0.0).then_inc(pads_done, 1)
            nc.vector.memset(f32(k_stack[:, :, 3 * HD + 2:P]), 0.0).then_inc(pads_done, 1)
            nc.vector.memset(f32(k_stack[:, :, 3 * HD:3 * HD + 2]), 1.0).then_inc(pads_done, 1)
            nc.vector.memset(zeros[:], 0.0).then_inc(zeros_done, 1)
            nc.vector.tensor_copy(ident_bf[:], ident[:]).then_inc(masks_done, 1)
            dve.wait_ge(mask_loaded, 16)
            nc.vector.tensor_copy(later_bf[:], later[:]).then_inc(masks_done, 1)
            kT_copy(0, 0)
            for j in range(NT):
                row_top(0, j, ps=both_ps[j % 2])
            split_top(0)
            top_copy(0, 1)
            kT_copy(1, 1)

            def step(h, b):
                for j in range(NT):
                    if has(h, -1):
                        row_top(h + 1, j)
                    if j == 2 and has(h, 2):
                        y_copy(h - 2, b)
                if has(h, -1):
                    split_top(h + 1)
                    top_copy(h + 1, b)
                if has(h, -2):
                    kT_copy(h + 2, b)
            rounds(dve, step)

        @block.gpsimd
        def _(pool):
            def stack_low(g, b):
                pool.wait_ge(q_hi, g + 1)
                nc.gpsimd.tensor_tensor(q_stack[:, :, 2 * HD:3 * HD], qk[:, :, ds(g * HD, HD)], f32(q_stack[:, :, 0:HD]),
                                        ALU.subtract).then_inc(q_lo, 1)
                pool.wait_ge(k_hi, g + 1)
                nc.gpsimd.tensor_tensor(k_stack[:, :, HD:2 * HD], qk[:, :, ds(g * HD + D, HD)], f32(k_stack[:, :, 0:HD]),
                                        ALU.subtract).then_inc(k_lo, 1)

            stack_low(0, 0)
            stack_low(1, 1)

            def step(h, b):
                if has(h, 0):
                    if beyond(h, 2):
                        pool.wait_ge(o_made, h - 1)
                    nc.gpsimd.tensor_copy(v_head[b][:], vv[:, :, ds(h, 1), :].rearrange("p t a e -> p t (a e)")).then_inc(v_ready, 1)
                if has(h, -2):
                    stack_low(h + 2, b)
            rounds(pool, step)

        @block.sync
        def _(sp):
            sp.dma_start(later[:], io["later"]).then_inc(mask_loaded, 16)
            sp.wait_ge(zeros_done, 1)
            for s in range(NS):
                sp.dma_start(keep["sorted"][s * P:(s + 1) * P, :], zeros[:]).then_inc(cleared, 16)

            def place_top(g, b):
                sp.wait_ge(top_out, g + 1)
                for n in range(2):
                    sp.dma_start(f32(qT[b][3 * HD + n:3 * HD + n + 1, :]).rearrange("p (t c) -> p t c", t=NT),
                                 f32(minus_topT[n * NT:(n + 1) * NT, :])).then_inc(top_placed, 16)
            place_top(0, 0)

            def step(h, b):
                if has(h, -1):
                    place_top(h + 1, 1 - b)
            rounds(sp, step)
            sp.wait_ge(cleared, 16 * NS)


E_N = 4
DFF = 4 * D
NS = (T + E_N * (P - 1)) // P
FC = P
NC = DFF // FC
WU = KB * 2 * FC + D


def project_and_norm(nc, sem, io, keep):
    with ExitStack() as ctx:
        sb = lambda name, shape, dt=F32: ctx.enter_context(nc.sbuf_tensor(name, shape, dt))
        psum = lambda name, shape: ctx.enter_context(nc.psum_tensor(name, shape, F32))
        y, h2_all, logits, ident = keep["y"], keep["h2"], keep["logits"], keep["ident"]

        w_raw = sb("e_w_raw", [P, KB, D])
        w = [sb(f"e_w_{part}", [P, KB, D], F32R) for part in ("hi", "lo")]
        ln_w, ln_b = sb("e_ln_w", [P, D]), sb("e_ln_b", [P, D])
        router = sb("e_router", [P, KB, E_N])
        t_in = [sb(f"e_t{b}", [P, D]) for b in range(2)]
        x1_in = [sb(f"e_x1_{b}", [P, D]) for b in range(2)]
        y_in = [sb(f"e_y{b}", [P, D]) for b in range(2)]
        yT = [[sb(f"e_yT{b}_{part}", [P, KB, P], F32R) for part in ("hi", "lo")] for b in range(2)]
        x2 = [sb(f"e_x2_{b}", [P, D]) for b in range(2)]
        normed, scaled = sb("e_normed", [P, D]), sb("e_scaled", [P, D])
        h2 = [sb(f"e_h2_{b}", [P, D]) for b in range(2)]
        h2T = [sb(f"e_h2T{b}", [P, KB, P]) for b in range(2)]
        res = [sb(f"e_res{b}", [P, D]) for b in range(2)]
        moments, mv, rstd, spacer = sb("e_moments", [P, 6]), sb("e_mv", [P, 2]), sb("e_rstd", [P, 1]), sb("e_spacer", [P, 1])

        yT_ps = [psum(f"e_yT_ps{b}", [P, KB, P]) for b in range(2)]
        x_ps = [psum(f"e_x_ps{b}", [P, D]) for b in range(2)]
        h2T_ps = psum("e_h2T_ps", [P, KB, P])
        logit_ps = psum("e_logit_ps", [P, CH])

        w_loaded = [sem(f"e_w_loaded{k}") for k in range(KB)]
        small_loaded = sem("e_small_loaded")
        in_loaded = [sem(f"e_in_loaded{b}") for b in range(2)]
        res_stored = [sem(f"e_res_stored{b}") for b in range(2)]
        w_hi, w_lo = sem("e_w_hi"), sem("e_w_lo")
        y_copied, turned, yT_hi, yT_lo = sem("e_y_copied"), sem("e_turned"), sem("e_yT_hi"), sem("e_yT_lo")
        x_made, x2_done, moments_done, mv_done = sem("e_x_made"), sem("e_x2_done"), sem("e_moments_done"), sem("e_mv_done")
        var_done, rstd_done, normed_done, scaled_done = sem("e_var_done"), sem("e_rstd_done"), sem("e_normed_done"), sem("e_scaled_done")
        h2_done, res_done, h2_kept, h2_turned = sem("e_h2_done"), sem("e_res_done"), sem("e_h2_kept"), sem("e_h2_turned")
        h2T_out, logit_made, logit_out = sem("e_h2T_out"), sem("e_logit_made"), sem("e_logit_out")

        def rounds(eng, step):
            for i in range(4):
                step(i, i % 2)
            with eng.Fori(2, (NT - 3) // 2) as j:
                step(2 * j, 0)
                step(2 * j + 1, 1)
            for i in range(NT - 3, NT + 3):
                step(i, i % 2)

        def has(i, lag):
            return not isinstance(i, int) or 0 <= i - lag < NT

        def beyond(i, n):
            return not isinstance(i, int) or i >= n

        block = ctx.enter_context(nc.Block())

        @block.sync
        def _(sp):
            for k in range(KB):
                sp.dma_start(w_raw[:, k, :], io["proj_w"][k * P:(k + 1) * P, :]).then_inc(w_loaded[k], 16)
            sp.dma_start(ln_w[:], io["ln2_w"].partition_broadcast(P)).then_inc(small_loaded, 16)
            sp.dma_start(ln_b[:], io["ln2_b"].partition_broadcast(P)).then_inc(small_loaded, 16)
            sp.dma_start(router[:], io["router"]).then_inc(small_loaded, 16)
            sp.dma_start(keep["route_consts"][:], io["route_consts"]).then_inc(keep["consts_loaded"], 16)
            sp.dma_start(keep["tri"][:], io["tri"]).then_inc(keep["consts_loaded"], 16)

            def step(i, b):
                if has(i, 0):
                    if beyond(i, 2):
                        sp.wait_ge(x2_done, i - 1)
                        sp.wait_ge(res_done, i - 1)
                    sp.dma_start(t_in[b][:], keep["dram"]["t"][ds(i * P, P), :]).then_inc(in_loaded[b], 16)
                    sp.dma_start(x1_in[b][:], keep["dram"]["x1"][ds(i * P, P), :]).then_inc(in_loaded[b], 16)
                if has(i, 2):
                    sp.wait_ge(res_done, i - 1)
                    sp.dma_start(keep["dram"]["res"][ds((i - 2) * P, P), :], res[b][:]).then_inc(res_stored[b], 16)
            rounds(sp, step)
            for b in range(2):
                sp.wait_ge(res_stored[b], 16 * ((NT + 1 - b) // 2))

        @block.tensor
        def _(pe):
            def turn_y(t, b):
                pe.wait_ge(y_copied, t + 1)
                if beyond(t, 2):
                    pe.wait_ge(yT_lo, t - 1)
                for k in range(KB):
                    last = nc.tensor.transpose(yT_ps[b][:, k, :], y_in[b][:, k * P:(k + 1) * P], ident[:])
                last.then_inc(turned, 1)

            turn_y(0, 0)

            def step(i, b):
                if has(i, -1):
                    turn_y(i + 1, 1 - b)
                if has(i, 1):
                    if isinstance(i, int) and i == 1:
                        pe.wait_ge(w_lo, KB)
                    pe.wait_ge(yT_lo, i)
                    if beyond(i, 3):
                        pe.wait_ge(x2_done, i - 2)
                    for m, (k, (py, pw)) in enumerate((k, ps) for k in range(KB) for ps in PASSES):
                        last = nc.tensor.matmul(x_ps[1 - b][:], yT[1 - b][py][:, k, :], w[pw][:, k, :],
                                                start=(m == 0), stop=(m == 3 * KB - 1))
                    last.then_inc(x_made, 1)
                if has(i, 3):
                    if isinstance(i, int) and i == 3:
                        pe.wait_ge(small_loaded, 48)
                    pe.wait_ge(h2T_out, i - 2)
                    if beyond(i, 4):
                        pe.wait_ge(logit_out, i - 3)
                    for k in range(KB):
                        last = nc.tensor.matmul(logit_ps[:, 0:E_N], h2T[1 - b][:, k, :], router[:, k, :],
                                                start=(k == 0), stop=(k == KB - 1))
                    last.then_inc(logit_made, 1)
                if has(i, 2):
                    pe.wait_ge(h2_done, i - 1)
                    if beyond(i, 3):
                        pe.wait_ge(h2T_out, i - 2)
                    for k in range(KB):
                        last = nc.tensor.transpose(h2T_ps[:, k, :], h2[b][:, k * P:(k + 1) * P], ident[:])
                    last.then_inc(h2_turned, 1)
            rounds(pe, step)

        @block.scalar
        def _(act):
            def y_copy(t, b):
                if beyond(t, 2):
                    act.wait_ge(turned, t - 1)
                nc.scalar.copy(y_in[b][:].unsqueeze(1), y[:, ds(t, 1), :]).then_inc(y_copied, 1)

            def y_high(t, b):
                act.wait_ge(turned, t + 1)
                if beyond(t, 2):
                    act.wait_ge(x_made, t - 1)
                nc.scalar.copy(yT[b][0][:], yT_ps[b][:]).then_inc(yT_hi, 1)

            y_copy(0, 0)
            y_copy(1, 1)
            y_high(0, 0)

            def step(i, b):
                if has(i, -2):
                    y_copy(i + 2, b)
                if has(i, -1):
                    y_high(i + 1, 1 - b)
                if isinstance(i, int) and i == 0:
                    for k in range(KB):
                        act.wait_ge(w_loaded[k], 16)
                        nc.scalar.copy(w[0][:, k, :], w_raw[:, k, :]).then_inc(w_hi, 1)
                if isinstance(i, int) and i == 3:
                    for e in range(2):
                        act.dma_start(keep["w_raw"][e][:], io["moe_w"][e]).then_inc(keep["w_loaded"][e], 16)
                if isinstance(i, int) and i in (NT, NT + 1):
                    e = i - NT
                    act.wait_ge(keep["w_loaded"][e], 16)
                    nc.scalar.copy(keep["w"][0][0][:, e, :], keep["w_raw"][e][:]).then_inc(keep["w_hi"], 1)
                if has(i, 2):
                    act.wait_ge(h2_done, i - 1)
                    nc.scalar.copy(h2_all[:, ds(i - 2, 1), :], h2[b][:].unsqueeze(1)).then_inc(h2_kept, 1)
                    act.wait_ge(h2_turned, i - 1)
                    if beyond(i, 4):
                        act.wait_ge(logit_made, i - 3)
                    nc.scalar.copy(h2T[b][:], h2T_ps[:]).then_inc(h2T_out, 1)
            rounds(act, step)

        @block.vector
        def _(dve):
            def y_low(i, b):
                dve.wait_ge(yT_hi, i + 1)
                nc.vector.tensor_tensor(yT[b][1][:], yT_ps[b][:], f32(yT[b][0][:]), ALU.subtract).then_inc(yT_lo, 1)

            y_low(0, 0)

            def step(i, b):
                if has(i, -1) and not has(i, 1):
                    y_low(i + 1, 1 - b)
                if isinstance(i, int) and i == 0:
                    for k in range(KB):
                        dve.wait_ge(w_hi, k + 1)
                        nc.vector.tensor_tensor(w[1][:, k, :], w_raw[:, k, :], f32(w[0][:, k, :]), ALU.subtract).then_inc(w_lo, 1)
                    dve.wait_ge(small_loaded, 48)
                if has(i, 1):
                    o = 1 - b
                    dve.wait_ge(in_loaded[o], 32 * ((i - 1) // 2 + 1) if isinstance(i, int) else 16 * i + (16 if b else 0))
                    dve.wait_ge(x_made, i)
                    if beyond(i, 3):
                        dve.wait_ge(res_done, i - 2)
                    nc.vector.tensor_tensor(x2[o][:], x_ps[o][:], t_in[o][:], ALU.add).then_inc(x2_done, 1)
                    dve.wait_ge(x2_done, i)
                    nc.vector.bn_stats(moments[:], x2[o][:]).then_inc(moments_done, 1)
                    dve.wait_ge(moments_done, i)
                    nc.vector.memset(spacer[:], 0.0)
                    nc.vector.bn_aggr(mv[:], moments[:]).then_inc(mv_done, 1)
                    if has(i, -1):
                        y_low(i + 1, 1 - b)
                    dve.wait_ge(mv_done, i)
                    dve.wait_ge(rstd_done, i)
                    nc.vector.tensor_scalar(normed[:], x2[o][:], mv[:, 0:1], rstd[:], ALU.subtract, ALU.mult).then_inc(normed_done, 1)
                    dve.wait_ge(normed_done, i)
                    dve.wait_ge(h2_done, i - 1)
                    nc.vector.tensor_tensor(scaled[:], normed[:], ln_w[:], ALU.mult).then_inc(scaled_done, 1)
                    dve.wait_ge(scaled_done, i)
                    if beyond(i, 3):
                        dve.wait_ge(h2_turned, i - 2)
                        dve.wait_ge(h2_kept, i - 2)
                    nc.vector.tensor_tensor(h2[o][:], scaled[:], ln_b[:], ALU.add).then_inc(h2_done, 1)
                if has(i, 3):
                    dve.wait_ge(logit_made, i - 2)
                    nc.vector.tensor_copy(logits[:, :, ds(i - 3, 1)], logit_ps[:, 0:E_N].unsqueeze(2)).then_inc(logit_out, 1)
            rounds(dve, step)

        @block.gpsimd
        def _(pool):
            def step(i, b):
                if has(i, 1):
                    o = 1 - b
                    pool.wait_ge(mv_done, i)
                    nc.gpsimd.tensor_tensor(mv[:, 1:2], mv[:, 1:2], keep["eps"][:], ALU.add).then_inc(var_done, 1)
                    pool.wait_ge(var_done, i)
                    nc.gpsimd.tensor_tensor(rstd[:], mv[:, 1:2], keep["minus_half"][:], ALU.pow).then_inc(rstd_done, 1)
                    if not isinstance(i, int):
                        pool.wait_ge(res_stored[o], 8 * i - (16 if b == 0 else 8))
                    elif i >= 3:
                        pool.wait_ge(res_stored[o], 16 * ((i - 1) // 2))
                    pool.wait_ge(in_loaded[o], 32 * ((i - 1) // 2 + 1) if isinstance(i, int) else 16 * i + (16 if b else 0))
                    nc.gpsimd.tensor_tensor(res[o][:], x2[o][:], x1_in[o][:], ALU.add).then_inc(res_done, 1)
            rounds(pool, step)


def route(nc, sem, io, keep):
    with ExitStack() as ctx:
        sb = lambda name, shape, dt=F32: ctx.enter_context(nc.sbuf_tensor(name, shape, dt))
        psum = lambda name, shape: ctx.enter_context(nc.psum_tensor(name, shape, F32))
        logits = keep["logits"]

        consts = keep["route_consts"]
        tri = keep["tri"]
        best = sb("f_best", [P, NT])
        equal = sb("f_equal", [P, E_N, NT])
        seen = [sb(f"f_seen{n}", [P, NT]) for n in range(3)]
        first = sb("f_first", [P, E_N, NT])
        hot = sb("f_hot", [P, E_N, NT])
        counts = sb("f_counts", [P, 2, E_N, NT])
        upto = sb("f_upto", [P, E_N, NT])
        more = sb("f_more", [P, E_N, NT])
        tiles = sb("f_tiles", [P, E_N])
        ends = sb("f_ends", [P, E_N])
        starts = sb("f_starts", [P, E_N])
        place = [sb(f"f_place{n}", [P, E_N, NT]) for n in range(4)]
        slot_f = sb("f_slot_f", [P, NT])
        passed = sb("f_passed", [P, E_N - 1, NS])
        expert = [sb(f"f_expert{n}", [P, NS]) for n in range(2)]

        count_ps = psum("f_count_ps", [P, CH])

        consts_loaded, link_done, hot_done = keep["consts_loaded"], sem("f_link_done"), sem("f_hot_done")
        counted, slots_done, scattered = sem("f_counted"), sem("f_slots_done"), sem("f_scattered")

        block = ctx.enter_context(nc.Block())

        @block.sync
        def _(sp):
            sp.wait_ge(scattered, 16 * NT)

        @block.scalar
        def _(act):
            for e in range(2, E_N):
                act.wait_ge(keep["w_lo"], e - 1)
                act.dma_start(keep["w_raw"][e % 2][:], io["moe_w"][e]).then_inc(keep["w_loaded"][e % 2], 16)
            for e in range(2, E_N):
                act.wait_ge(keep["w_loaded"][e % 2], 32)
                nc.scalar.copy(keep["w"][0][0][:, e, :], keep["w_raw"][e % 2][:]).then_inc(keep["w_hi"], 1)

        @block.gpsimd
        def _(pool):
            for e in range(2):
                pool.wait_ge(keep["w_hi"], e + 1)
                nc.gpsimd.tensor_tensor(keep["w"][0][1][:, e, :], keep["w_raw"][e][:], f32(keep["w"][0][0][:, e, :]),
                                        ALU.subtract).then_inc(keep["w_lo"], 1)
            pool.wait_ge(slots_done, 1)
            for t in range(NT):
                rows = P if t < NT - 1 else TL
                nc.gpsimd.indirect_dma_start(keep["sorted"], bass.IndirectOffsetOnAxis(ap=keep["slot"][0:rows, t:t + 1], axis=0),
                                             keep["h2"][0:rows, t, :], None).then_inc(scattered, 16)

        @block.tensor
        def _(pe):
            pe.wait_ge(consts_loaded, 32)
            pe.wait_ge(hot_done, 1)
            for n in range(2):
                last = nc.tensor.matmul(count_ps[:, n * E_N * NT:(n + 1) * E_N * NT], tri[:, n, :],
                                        hot[:].rearrange("p e t -> p (e t)"), start=True, stop=True)
            last.then_inc(counted, 1)

        @block.vector
        def _(dve):
            links = [0]

            def link(instruction):
                links[0] += 1
                instruction.then_inc(link_done, 1)
                dve.wait_ge(link_done, links[0])

            valid, carry, threshold, number = (consts[:, n] for n in range(4))
            dve.wait_ge(consts_loaded, 32)
            link(nc.vector.tensor_reduce(best[:], logits[:].rearrange("p e t -> p t e"), AX.X, ALU.max))
            link(nc.vector.tensor_tensor(equal[:], logits[:], best[:].unsqueeze(1).to_broadcast([P, E_N, NT]), ALU.is_equal))
            nc.vector.tensor_copy(first[:, 0, :], equal[:, 0, :])
            link(nc.vector.tensor_copy(seen[0][:], equal[:, 0, :]))
            for e in range(1, E_N):
                if e < E_N - 1:
                    nc.vector.tensor_tensor(seen[e][:], seen[e - 1][:], equal[:, e, :], ALU.max)
                link(nc.vector.tensor_tensor(first[:, e, :], equal[:, e, :], seen[e - 1][:], ALU.is_gt))
            nc.vector.tensor_tensor(hot[:], first[:], valid[:, :, 0:NT], ALU.mult).then_inc(hot_done, 1)
            dve.wait_ge(counted, 1)
            link(nc.vector.tensor_copy(counts[:].rearrange("p n e t -> p (n e t)"), count_ps[:, 0:2 * E_N * NT]))
            for e in range(E_N):
                last = nc.vector.tensor_tensor_scan(upto[:, e, :], carry[:, e, 0:NT], counts[:, 1, e, :], 0.0, ALU.mult, ALU.add)
            link(last)
            link(nc.vector.tensor_tensor(more[:], threshold[:, :, 0:NT], upto[:, :, NT - 1:NT].to_broadcast([P, E_N, NT]), ALU.is_lt))
            link(nc.vector.tensor_reduce(tiles[:], more[:], AX.X, ALU.add))
            link(nc.vector.tensor_tensor_scan(ends[:], carry[:, 0, 1:1 + E_N], tiles[:], 0.0, ALU.mult, ALU.add))
            link(nc.vector.tensor_tensor(starts[:], ends[:], tiles[:], ALU.subtract))
            link(nc.vector.tensor_tensor(place[0][:], upto[:], counts[:, 1], ALU.subtract))
            link(nc.vector.tensor_tensor(place[1][:], place[0][:], counts[:, 0], ALU.add))
            link(nc.vector.scalar_tensor_tensor(place[2][:], starts[:].unsqueeze(2).to_broadcast([P, E_N, NT]), float(P),
                                                place[1][:], ALU.mult, ALU.add))
            link(nc.vector.tensor_tensor(place[3][:], place[2][:], hot[:], ALU.mult))
            link(nc.vector.tensor_reduce(slot_f[:], place[3][:].rearrange("p e t -> p t e"), AX.X, ALU.add))
            nc.vector.tensor_copy(keep["slot"][:], slot_f[:]).then_inc(slots_done, 1)
            link(nc.vector.tensor_tensor(passed[:], number[:, 0:E_N - 1, :], ends[:, 0:E_N - 1].unsqueeze(2).to_broadcast([P, E_N - 1, NS]),
                                         ALU.is_ge))
            link(nc.vector.tensor_reduce(expert[0][:], passed[:].rearrange("p e s -> p s e"), AX.X, ALU.add))
            link(nc.vector.tensor_scalar(expert[1][:], expert[0][:], float(WU), None, ALU.mult))
            nc.vector.tensor_copy(keep["w_at"][:], expert[1][:]).then_inc(keep["w_at_done"], 1)
            for e in range(2, E_N):
                dve.wait_ge(keep["w_hi"], e + 1)
                nc.vector.tensor_tensor(keep["w"][0][1][:, e, :], keep["w_raw"][e % 2][:], f32(keep["w"][0][0][:, e, :]),
                                        ALU.subtract).then_inc(keep["w_lo"], 1)


def experts(nc, sem, io, keep):
    with ExitStack() as ctx:
        sb = lambda name, shape, dt=F32: ctx.enter_context(nc.sbuf_tensor(name, shape, dt))
        psum = lambda name, shape: ctx.enter_context(nc.psum_tensor(name, shape, F32))
        sT, w, w_raw, ident = keep["sT"], keep["w"], keep["w_raw"], keep["ident"]
        w_loaded, w_hi, w_lo = keep["w_loaded"], keep["w_hi"], keep["w_lo"]

        y = sb("g_y", [P, NS, D])
        sig = [sb(f"g_sig{b}", [P, FC]) for b in range(2)]
        silu = [sb(f"g_silu{b}", [P, FC]) for b in range(2)]
        a = [sb(f"g_a{b}", [P, FC]) for b in range(2)]
        aT = [[sb(f"g_aT{b}_{part}", [P, P], F32R) for part in ("hi", "lo")] for b in range(2)]

        gv_ps = [psum(f"g_gv_ps{b}", [P, CH]) for b in range(2)]
        aT_ps = [psum(f"g_aT_ps{b}", [P, CH]) for b in range(2)]
        y_ps = [psum(f"g_y_ps{b}", [P, D]) for b in range(2)]
        sT_ps = [psum(f"g_sT_ps{b}", [P, KB, P]) for b in range(2)]

        gv_made, sig_done, silu_done, a_done = sem("g_gv_made"), sem("g_sig_done"), sem("g_silu_done"), sem("g_a_done")
        turned, aT_hi, aT_lo = sem("g_turned"), sem("g_aT_hi"), sem("g_aT_lo")
        y_made, y_added, chunk_done, y_stored = sem("g_y_made"), sem("g_y_added"), sem("g_chunk_done"), sem("g_y_stored")
        res_loaded = sem("g_res_loaded")
        s_loaded = [sem(f"g_s_loaded{s}") for s in range(NS)]
        s_turned, sT_hi, sT_lo = sem("g_s_turned"), sem("g_sT_hi"), sem("g_sT_lo")

        assert NS % 2 == 0 and NC % 2 == 0
        LOOP = NC // 2
        PER = 2 * NS
        SPLIT_AT = {3: 0, 5: 1, 7: 2, 9: 3}

        def pairs(eng, step):
            for r in range(PER):
                step(0, r)
            with eng.Fori(1, LOOP - 1) as it:
                for r in range(PER):
                    step(it, r)
            for r in range(PER):
                step(LOOP - 1, r)

        def started(it, r, lag):
            return not isinstance(it, int) or PER * it + r >= lag

        def first_chunk(it, r):
            return isinstance(it, int) and it == 0 and r < NS

        def following(it, r):
            return not isinstance(it, int) or 2 * it + r // NS + 1 < NC

        block = ctx.enter_context(nc.Block())

        @block.tensor
        def _(pe):
            pe.wait_ge(keep["w_at_done"], 1)

            def read_place(s):
                return pe.value_load(keep["w_at"][0:1, s:s + 1], min_val=0, max_val=(E_N - 1) * WU)

            places = {}

            def turn_rows(s):
                pe.wait_ge(s_loaded[s], 16)
                if s >= 2:
                    pe.wait_ge(sT_lo, s - 1)
                for k in range(KB):
                    last = nc.tensor.transpose(sT_ps[s % 2][:, k, :], y[:, s, k * P:(k + 1) * P], ident[:])
                last.then_inc(s_turned, 1)

            def gate_value(it, r):
                u, b, c, s = PER * it + r, r % 2, r // NS, r % NS
                if first_chunk(it, r):
                    pe.wait_ge(sT_lo, s + 1)
                at = places[r] = read_place(s)
                if s == 0:
                    pe.wait_ge(w_hi, E_N * (2 * it + c + 1))
                    pe.wait_ge(w_lo, E_N * (2 * it + c + 1))
                for m, (k, (ps, pw)) in enumerate((k, p) for k in range(KB) for p in PASSES):
                    weights = w[c][pw][:].rearrange("p e n -> p (e n)")[:, ds(at + k * 2 * FC, 2 * FC)]
                    last = nc.tensor.matmul(gv_ps[b][:, 0:2 * FC], sT[ps][:, s, k, :], weights, start=(m == 0), stop=(m == 3 * KB - 1))
                last.then_inc(gv_made, 1)

            def turn(it, r):
                u, b = PER * it + r, (r - 1) % 2
                pe.wait_ge(a_done, u)
                nc.tensor.transpose(aT_ps[b][:, 0:P], a[b][:], ident[:]).then_inc(turned, 1)

            def project(it, r):
                u, b, c, s = PER * it + r, r % 2, (r - 2) // NS % 2, (r - 2) % NS
                at = places.pop(r - 2) if r >= 2 else read_place(s)
                pe.wait_ge(aT_lo, u - 1)
                if started(it, r, 4):
                    pe.wait_ge(y_added, u - 3)
                for m, (pa, pw) in enumerate(PASSES):
                    weights = w[c][pw][:].rearrange("p e n -> p (e n)")[:, ds(at + KB * 2 * FC, D)]
                    last = nc.tensor.matmul(y_ps[b][:], aT[b][pa][:], weights, start=(m == 0), stop=(m == 2))
                last.then_inc(chunk_done if s == NS - 1 else y_made, 1)

            turn_rows(0)
            turn_rows(1)

            def step(it, r):
                gate_value(it, r)
                if first_chunk(it, r) and r + 2 < NS:
                    turn_rows(r + 2)
                if started(it, r, 1):
                    turn(it, r)
                if started(it, r, 2):
                    project(it, r)
            pairs(pe, step)
            turn(LOOP, 0)
            project(LOOP, 0)
            project(LOOP, 1)

        @block.scalar
        def _(act):
            def turn_high(it, r):
                u, b = PER * it + r, (r - 1) % 2
                act.wait_ge(turned, u)
                if started(it, r, 3):
                    act.wait_ge(aT_used(it, r), aT_used_count(it, r))
                nc.scalar.copy(aT[b][0][:], aT_ps[b][:, 0:P]).then_inc(aT_hi, 1)

            def aT_used(it, r):
                return chunk_done if (r - 3) % NS == NS - 1 else y_made

            def aT_used_count(it, r):
                chunks_before = 2 * it + (r - 3) // NS
                if (r - 3) % NS == NS - 1:
                    return chunks_before + 1
                return chunks_before * (NS - 1) + (r - 3) % NS + 1

            def rows_high(s):
                act.wait_ge(s_turned, s + 1)
                nc.scalar.copy(sT[0][:, s, :, :], sT_ps[s % 2][:]).then_inc(sT_hi, 1)

            rows_high(0)
            rows_high(1)

            def step(it, r):
                u, b = PER * it + r, r % 2
                act.wait_ge(gv_made, u + 1)
                if started(it, r, 2):
                    act.wait_ge(silu_done, u - 1)
                nc.scalar.activation(sig[b][:], gv_ps[b][:, 0:FC], ACT.Sigmoid).then_inc(sig_done, 1)
                if first_chunk(it, r) and r + 2 < NS:
                    rows_high(r + 2)
                if started(it, r, 1):
                    turn_high(it, r)
                if r % NS in SPLIT_AT and following(it, r):
                    c, e = r // NS, SPLIT_AT[r % NS]
                    act.wait_ge(chunk_done, 2 * it + c)
                    act.wait_ge(w_loaded[e % 2], 16 * (2 * (2 * it + c + 1) + e // 2 + 1))
                    nc.scalar.copy(w[1 - c][0][:, e, :], w_raw[e % 2][:]).then_inc(w_hi, 1)
            pairs(act, step)
            turn_high(LOOP, 0)

        @block.gpsimd
        def _(pool):
            def chunk(it, c):
                for e in range(E_N):
                    pool.wait_ge(w_hi, E_N * (2 * it + c + 1) + e + 1)
                    nc.gpsimd.tensor_tensor(w[1 - c][1][:, e, :], w_raw[e % 2][:], f32(w[1 - c][0][:, e, :]), ALU.subtract).then_inc(w_lo, 1)
            with pool.Fori(0, LOOP - 1) as it:
                chunk(it, 0)
                chunk(it, 1)
            chunk(LOOP - 1, 0)

        @block.sync
        def _(sp):
            for s in range(NS):
                sp.dma_start(y[:, s, :], keep["sorted"][s * P:(s + 1) * P, :]).then_inc(s_loaded[s], 16)

            def chunk(c):
                for e in range(E_N):
                    sp.wait_ge(w_lo, E_N * (c + 1) + e - 1)
                    sp.dma_start(w_raw[e % 2][:], io["moe_w"][ds((c + 1) * E_N + e, 1)].rearrange("a p n -> (a p) n")).then_inc(w_loaded[e % 2], 16)
            with sp.Fori(0, NC - 1) as c:
                chunk(c)
            sp.wait_ge(chunk_done, NC - 1)
            sp.dma_start(keep["res_in"], keep["dram"]["res"].rearrange("(t p) d -> p t d", p=P)).then_inc(res_loaded, 16)
            for s in range(NS):
                sp.wait_ge(y_added, (NC - 1) * NS + s + 1)
                sp.dma_start(keep["sorted"][s * P:(s + 1) * P, :], y[:, s, :]).then_inc(y_stored, 16)
            sp.wait_ge(y_stored, 16 * NS)
            sp.wait_ge(res_loaded, 16)

        @block.vector
        def _(dve):
            def turn_low(it, r):
                u, b = PER * it + r, (r - 1) % 2
                dve.wait_ge(aT_hi, u)
                nc.vector.tensor_tensor(aT[b][1][:], aT_ps[b][:, 0:P], f32(aT[b][0][:]), ALU.subtract).then_inc(aT_lo, 1)

            def add(it, r):
                b, s = r % 2, (r - 2) % NS
                chunks_before = 2 * it + (r - 2) // NS
                if s == NS - 1:
                    dve.wait_ge(chunk_done, chunks_before + 1)
                else:
                    dve.wait_ge(y_made, chunks_before * (NS - 1) + s + 1)
                if isinstance(it, int) and chunks_before == 0:
                    nc.vector.tensor_copy(y[:, s, :], y_ps[b][:]).then_inc(y_added, 1)
                else:
                    nc.vector.tensor_tensor(y[:, s, :], y_ps[b][:], y[:, s, :], ALU.add).then_inc(y_added, 1)

            def rows_low(s):
                dve.wait_ge(sT_hi, s + 1)
                nc.vector.tensor_tensor(sT[1][:, s, :, :], sT_ps[s % 2][:], f32(sT[0][:, s, :, :]), ALU.subtract).then_inc(sT_lo, 1)

            rows_low(0)
            rows_low(1)

            def step(it, r):
                u, b = PER * it + r, r % 2
                dve.wait_ge(sig_done, u + 1)
                nc.vector.tensor_tensor(silu[b][:], gv_ps[b][:, 0:FC], sig[b][:], ALU.mult).then_inc(silu_done, 1)
                dve.wait_ge(silu_done, u + 1)
                if started(it, r, 2):
                    dve.wait_ge(turned, u - 1)
                nc.vector.tensor_tensor(a[b][:], gv_ps[b][:, FC:2 * FC], silu[b][:], ALU.mult).then_inc(a_done, 1)
                if first_chunk(it, r) and r + 2 < NS:
                    rows_low(r + 2)
                if started(it, r, 1):
                    turn_low(it, r)
                if started(it, r, 2):
                    add(it, r)
            pairs(dve, step)
            turn_low(LOOP, 0)
            add(LOOP, 0)
            add(LOOP, 1)


def combine(nc, sem, io, keep, out):
    with ExitStack() as ctx:
        got = [ctx.enter_context(nc.sbuf_tensor(f"h_got{t}", [P, D], F32)) for t in range(NT)]
        res = keep["res_in"]
        gathered = [sem(f"h_gathered{t}") for t in range(NT)]
        summed, stored = sem("h_summed"), sem("h_stored")
        block = ctx.enter_context(nc.Block())

        @block.gpsimd
        def _(pool):
            for t in range(NT):
                rows = P if t < NT - 1 else TL
                nc.gpsimd.indirect_dma_start(got[t][0:rows, :], None, keep["sorted"],
                                             bass.IndirectOffsetOnAxis(ap=keep["slot"][0:rows, t:t + 1], axis=0)).then_inc(gathered[t], 16)

        @block.vector
        def _(dve):
            for t in range(NT):
                rows = P if t < NT - 1 else TL
                dve.wait_ge(gathered[t], 16)
                nc.vector.tensor_tensor(got[t][0:rows, :], got[t][0:rows, :], res[0:rows, t, :], ALU.add).then_inc(summed, 1)

        @block.sync
        def _(sp):
            for t in range(NT):
                rows = P if t < NT - 1 else TL
                sp.wait_ge(summed, t + 1)
                sp.dma_start(out[t * P:t * P + rows, :], got[t][0:rows, :]).then_inc(stored, 16)
            sp.wait_ge(stored, 16 * NT)


def phase(nc, build, io, keep, *rest):
    used = []

    def sem(name):
        used.append(nc.alloc_semaphore(name=name))
        return used[-1]
    build(nc, sem, io, keep, *rest)
    nc.clear_and_free_semaphores(used)
    nc.all_engine_barrier()


def program(nc, io, out):
    with ExitStack() as top:
        sem = lambda name: top.enter_context(nc.semaphore(name))
        sb = lambda ctx: lambda name, shape, dt=F32: ctx.enter_context(nc.sbuf_tensor(name, shape, dt))
        small = sb(top)
        keep = {
            "ident": small("ident", [P, P]), "minus_half": small("minus_half", [P, 1]), "eps": small("eps", [P, 1]),
            "logits": small("logits", [P, E_N, NT]), "slot": small("slot", [P, NT], U32), "w_at": small("w_at", [P, NS], I32),
            "ident_loaded": sem("ident_loaded"), "const_done": sem("const_done"), "pad_cleared": sem("pad_cleared"),
            "rope_loaded": sem("rope_loaded"), "w_at_done": sem("w_at_done"), "consts_loaded": sem("consts_loaded"),
            "attn_w_loaded": [sem(f"attn_w_loaded{k}") for k in range(KB)],
            "w_loaded": [sem(f"w_loaded{b}") for b in range(2)], "w_hi": sem("w_hi"), "w_lo": sem("w_lo"),
            "dram": {name: nc.dram_tensor(f"kept_{name}", (TP, D), F32).ap() for name in ("x1", "t", "g", "res")},
            "sorted": nc.dram_tensor("sorted_rows", (NS * P, D), F32).ap(),
        }
        right = lambda ctx: lambda name, shape, dt=F32: ctx.enter_context(nc.sbuf_tensor(name, shape, dt, side="right"))
        early = ExitStack()
        with ExitStack() as ctx:
            keep["qT"] = sb(ctx)("qT", [P, KB, TP])
            keep["kT"] = [sb(ctx)(f"kT_{part}", [P, KB, TP], F32R) for part in ("hi", "lo")]
            keep["v"] = [sb(ctx)(f"v_{part}", [P, NT, D], F32R) for part in ("hi", "lo")]
            phase(nc, gnn_projections, io, keep)
            keep["attn_w_raw"] = [right(early)(f"attn_w_raw{k}", [P, 3 * D]) for k in range(KB - 1)]
            phase(nc, graph_attention, io, keep)
        with ExitStack() as weights, ExitStack() as rows:
            with ExitStack() as ctx:
                keep["y"] = sb(ctx)("y", [P, NT, D])
                with ExitStack() as heads:
                    keep["qk"] = sb(heads)("qk", [P, NT, 2 * D])
                    keep["vv"] = sb(heads)("vv", [P, NT, H, HV])
                    phase(nc, ffn_projections, io, keep)
                    early.close()
                    phase(nc, causal_attention, io, keep)
                first_w = [right(weights)(f"w0_{part}", [P, E_N, WU], F32R) for part in ("hi", "lo")]
                keep["w"] = [first_w]
                keep["w_raw"] = [right(weights)(f"w_raw{b}", [P, WU]) for b in range(2)]
                keep["h2"] = right(rows)("h2", [P, NT, D])
                keep["route_consts"] = right(rows)("route_consts", [P, 4, E_N, NS])
                keep["tri"] = right(rows)("tri", [P, 2, P])
                phase(nc, project_and_norm, io, keep)
            with ExitStack() as ctx:
                keep["sT"] = [sb(ctx)(f"sT_{part}", [P, NS, KB, P], F32R) for part in ("hi", "lo")]
                keep["w"].append([sb(ctx)(f"w1_{part}", [P, E_N, WU], F32R) for part in ("hi", "lo")])
                phase(nc, route, io, keep)
                rows.close()
                keep["res_in"] = f32(keep["w"][0][0][:]).rearrange("p e n -> p (e n)")[:, 0:NT * D].rearrange("p (t d) -> p t d", d=D)
                phase(nc, experts, io, keep)
                phase(nc, combine, io, keep, out)


def kernel(**inputs):
    import concourse.bacc as bacc
    from concourse.bass_utils import run_bass_kernel_spmd

    a = {name: np.asarray(value) for name, value in inputs.items()}

    def filled(x, rows):
        y = np.zeros((rows,) + x.shape[1:], x.dtype)
        y[:x.shape[0]] = x
        return y

    def columns(x):
        return np.ascontiguousarray(x.reshape(-1, P).T)

    def rope_tables():
        inv_freq = (1.0 / np.float32(10000.0) ** (np.arange(0, HD, 2, dtype=np.float32) / np.float32(HD))).astype(np.float32)
        freqs = np.arange(TP, dtype=np.float32)[:, None] * inv_freq[None, :]
        both = np.concatenate([freqs, freqs], -1)
        sign = np.where(np.arange(HD) < HD // 2, -1.0, 1.0).astype(np.float32)
        tables = np.stack([np.cos(both), np.sin(both) * sign]).astype(np.float32)
        return np.ascontiguousarray(tables.reshape(2, NT, P, HD).transpose(2, 0, 1, 3))

    def expert_chunks():
        wv = a["L0_ffn_expert_wv"].reshape(E_N, KB, P, 2, NC, FC).transpose(4, 0, 2, 1, 3, 5).reshape(NC, E_N, P, KB * 2 * FC)
        proj = a["L0_ffn_expert_proj"].reshape(E_N, NC, FC, D).transpose(1, 0, 2, 3)
        return np.ascontiguousarray(np.concatenate([wv, proj], -1).reshape(NC * E_N, P, WU))

    def route_constants():
        index = np.arange(NS)
        consts = np.zeros((P, 4, E_N, NS), np.float32)
        consts[:, 0] = (index[None, :] * P + np.arange(P)[:, None] < T)[:, None, :]
        consts[:, 1] = index > 0
        consts[:, 2] = index * P
        consts[:, 3] = index
        return consts

    arrays = {
        "x": filled(a["x"], TP),
        "adj": filled(a["adj"], TP),
        "w_q": np.ascontiguousarray(a["L0_gnn_W_q"].T),
        "w_k": np.ascontiguousarray(a["L0_gnn_W_k"].T),
        "w_v": np.ascontiguousarray(a["L0_gnn_W_v"].T),
        "b_q": columns(a["L0_gnn_b_q"]),
        "b_k": columns(a["L0_gnn_b_k"]),
        "b_v": a["L0_gnn_b_v"],
        "ident": np.eye(P, dtype=np.float32),
        "ln1_w": columns(a["L0_ffn_ln1_w"]),
        "ln1_b": columns(a["L0_ffn_ln1_b"]),
        "conv_w": np.ascontiguousarray(a["L0_ffn_conv_w"][:, 0, :].reshape(KB, P, 3).transpose(1, 0, 2)),
        "attn_w": a["L0_ffn_attn_w"],
        "rope": rope_tables(),
        "later": np.stack([np.where(np.arange(P)[None, :] > np.arange(P)[:, None], np.float32(-1e30), np.float32(0)),
                           np.where(np.arange(P)[:, None] > np.arange(P)[None, :], np.float32(-1e30), np.float32(0))], 1),
    }
    arrays.update({
        "proj_w": a["L0_ffn_proj_w"],
        "ln2_w": a["L0_ffn_ln2_w"],
        "ln2_b": a["L0_ffn_ln2_b"],
        "router": np.ascontiguousarray(a["L0_ffn_router_w"].reshape(KB, P, E_N).transpose(1, 0, 2)),
        "moe_w": expert_chunks(),
        "route_consts": route_constants(),
        "tri": np.stack([np.triu(np.ones((P, P), np.float32), 1), np.ones((P, P), np.float32)], 1),
    })
    nc = bacc.Bacc("TRN2", target_bir_lowering=False, num_devices=1)
    io = {n: nc.dram_tensor(f"in_{n}", x.shape, mybir.dt.from_np(x.dtype), kind="ExternalInput").ap() for n, x in arrays.items()}
    out = nc.dram_tensor("out", (T, D), F32, kind="ExternalOutput").ap()
    program(nc, io, out)
    r = run_bass_kernel_spmd(nc, [{f"in_{n}": x for n, x in arrays.items()}], core_ids=[0])
    return r.results[0]["out"]
```
